# Optimizing a Trainium2 kernel written in Bass

```python
import numpy as np
import jax
import jax.numpy as jnp

def _softmax(x, axis=-1):
    return jax.nn.softmax(x, axis=axis)

def _gelu(x):
    return jax.nn.gelu(x, approximate=True)

def _silu(x):
    return jax.nn.silu(x)

def _sigmoid(x):
    return jax.nn.sigmoid(x)

def _layernorm(x, axis=-1, eps=1e-05):
    m = jnp.mean(x, axis=axis, keepdims=True)
    v = jnp.var(x, axis=axis, keepdims=True)
    return (x - m) / jnp.sqrt(v + eps)

def _scatter_add(tgt, idx, src, axis=0):
    return tgt.at[idx].add(src)

def _segment_sum(src, seg, n):
    return jax.ops.segment_sum(src, seg, n)
kernel_name = 'mk_xattn_ffn_d2_seqx_r8_9ae9b9'

def setup_inputs(seed: int=0):
    np.random.seed(seed)
    _w = jnp.asarray

    def _rec_inputs():
        import jax
        import jax.numpy as jnp
        _rk = jax.random.key(seed)
        x = -0.0002928 + 1 * jax.random.normal(jax.random.fold_in(_rk, 1), (8, 128, 128), jnp.float32)
        _lenS = 128 - jax.random.randint(jax.random.fold_in(_rk, 7), (8,), 0, max(1, 128 // 4) + 1, jnp.int32)
        _lenS2 = 128 - jax.random.randint(jax.random.fold_in(_rk, 8), (8,), 0, max(1, 128 // 4) + 1, jnp.int32)
        _ctx_1024P = jax.random.normal(jax.random.fold_in(_rk, 11), (8, 16, 128), jnp.float32)
        _ctx_1024c = jax.random.dirichlet(jax.random.fold_in(_rk, 511), 0.3 * jnp.ones((16,), jnp.float32), (8, 128))
        _ctx_1024t = jnp.einsum('bsk,bkd->bsd', _ctx_1024c, _ctx_1024P)
        _ctx_1024t = _ctx_1024t * jax.lax.rsqrt(jnp.mean(jnp.square(_ctx_1024t)) + 1e-12) * 0.953939
        ctx_1024 = -1.39393e-06 + 0.999914 * (_ctx_1024t + 0.3 * jax.random.normal(jax.random.fold_in(_rk, 611), (8, 128, 128), jnp.float32))
        _validS = jnp.arange(128)[None, :] < _lenS[:, None]
        _validS2 = jnp.arange(128)[None, :] < _lenS2[:, None]
        _causal = jnp.tril(jnp.ones((128, 128), dtype=bool))
        mask_1x1xSxS2_bk1 = jnp.broadcast_to(_validS2[0:1, None, None, :], (1, 1, 128, 128))
        return (x, ctx_1024, mask_1x1xSxS2_bk1)
    x, ctx_1024, mask_1x1xSxS2_bk1 = _rec_inputs()

    def _L0_xattn_setup():
        import jax, jax.numpy as jnp
        import numpy as np
        import math
        D_MODEL = 128
        NUM_HEADS = 16
        D_K = D_MODEL // NUM_HEADS
        SEQ = 512
        BATCH = 1
        NUM_BUCKETS = 32
        MAX_DISTANCE = 512

        def _relative_position_bucket(relative_position):
            n = jnp.maximum(-relative_position, 0)
            max_exact = NUM_BUCKETS // 2
            is_small = n < max_exact
            nf = jnp.maximum(n, 1).astype(jnp.float32)
            val_if_large = max_exact + (jnp.log(nf / max_exact) / math.log(MAX_DISTANCE / max_exact) * (NUM_BUCKETS - max_exact)).astype(jnp.int32)
            val_if_large = jnp.minimum(val_if_large, NUM_BUCKETS - 1)
            return jnp.where(is_small, n, val_if_large)
        key = jax.random.key(seed)
        ks = jax.random.split(key, 12)
        s = 1.0 / math.sqrt(D_MODEL)
        inp = {'query': jax.random.normal(ks[0], (BATCH, SEQ, D_MODEL), jnp.float32), 'key': jax.random.normal(ks[1], (BATCH, SEQ, D_MODEL), jnp.float32), 'value': jax.random.normal(ks[2], (BATCH, SEQ, D_MODEL), jnp.float32), 'mask': jnp.triu(jnp.ones((SEQ, SEQ), bool), k=1)[None, None], 'Wq': jax.random.normal(ks[3], (D_MODEL, D_MODEL), jnp.float32) * s, 'bq': jnp.zeros((D_MODEL,), jnp.float32), 'Wk': jax.random.normal(ks[4], (D_MODEL, D_MODEL), jnp.float32) * s, 'bk': jnp.zeros((D_MODEL,), jnp.float32), 'Wv': jax.random.normal(ks[5], (D_MODEL, D_MODEL), jnp.float32) * s, 'bv': jnp.zeros((D_MODEL,), jnp.float32), 'Wo': jax.random.normal(ks[6], (D_MODEL, D_MODEL), jnp.float32) * s, 'bo': jnp.zeros((D_MODEL,), jnp.float32), 'rpe_table': jax.random.normal(ks[7], (NUM_BUCKETS, NUM_HEADS), jnp.float32)}
        return inp
    _L0_xattn_all = _L0_xattn_setup()
    _L0_xattn_in = {k: v for k, v in _L0_xattn_all.items() if k in ('Wq', 'bq', 'Wk', 'bk', 'Wv', 'bv', 'Wo', 'bo', 'rpe_table')}
    del _L0_xattn_all

    def _L0_ffn_setup():
        import jax, jax.numpy as jnp
        import numpy as np
        D_MODEL, D_FF, RANK = (128, 512, 32)
        B, S = (4, 512)
        key = jax.random.key(seed)
        ks = jax.random.split(key, 7)
        return {'x': jax.random.normal(ks[0], (B, S, D_MODEL), dtype=jnp.float32), 'U1': jax.random.normal(ks[1], (D_MODEL, RANK), dtype=jnp.float32) * 0.02, 'V1': jax.random.normal(ks[2], (RANK, D_FF), dtype=jnp.float32) * 0.02, 'b1': jnp.zeros((D_FF,), dtype=jnp.float32), 'U2': jax.random.normal(ks[3], (D_FF, RANK), dtype=jnp.float32) * 0.02, 'V2': jax.random.normal(ks[4], (RANK, D_MODEL), dtype=jnp.float32) * 0.02, 'b2': jnp.zeros((D_MODEL,), dtype=jnp.float32)}
    _L0_ffn_all = _L0_ffn_setup()
    _L0_ffn_in = {k: v for k, v in _L0_ffn_all.items() if k in ('U1', 'V1', 'b1', 'U2', 'V2', 'b2')}
    del _L0_ffn_all

    def _L1_xattn_setup():
        import jax, jax.numpy as jnp
        import numpy as np
        N_HEAD = 16
        D_MODEL = 128
        D_K = D_MODEL // N_HEAD
        key = jax.random.key(seed)
        ks = jax.random.split(key, 11)
        B, S, D = (4, 256, D_MODEL)
        sc = 1.0 / np.sqrt(D)
        return {'Q': jax.random.normal(ks[0], (B, S, D), jnp.float32), 'K': jax.random.normal(ks[1], (B, S, D), jnp.float32), 'V': jax.random.normal(ks[2], (B, S, D), jnp.float32), 'Wq': jax.random.normal(ks[3], (N_HEAD, D, D_K), jnp.float32) * sc, 'bq': jnp.zeros((N_HEAD, D_K), jnp.float32), 'Wk': jax.random.normal(ks[4], (N_HEAD, D, D_K), jnp.float32) * sc, 'bk': jnp.zeros((N_HEAD, D_K), jnp.float32), 'Wv': jax.random.normal(ks[5], (N_HEAD, D, D_K), jnp.float32) * sc, 'bv': jnp.zeros((N_HEAD, D_K), jnp.float32), 'Wo': jax.random.normal(ks[6], (D, D), jnp.float32) * sc, 'bo': jnp.zeros((D,), jnp.float32)}
    _L1_xattn_all = _L1_xattn_setup()
    _L1_xattn_in = {k: v for k, v in _L1_xattn_all.items() if k in ('Wq', 'bq', 'Wk', 'bk', 'Wv', 'bv', 'Wo', 'bo')}
    del _L1_xattn_all

    def _L1_ffn_setup():
        import jax, jax.numpy as jnp
        import numpy as np
        B, L, D = (4, 128, 128)
        E, H, K = (16, 64, 8)
        EPS = 1e-12

        def _l2norm(v, axis=-1):
            n = jnp.sqrt(jnp.sum(v * v, axis=axis, keepdims=True))
            return v / jnp.maximum(n, EPS)
        if __name__ == '__main__':
            out = reference(**setup_inputs())
            print(out.shape)
        key = jax.random.key(seed)
        ks = jax.random.split(key, 8)
        s = lambda fan_in: 1.0 / np.sqrt(fan_in)
        return {'x': jax.random.normal(ks[0], (B, L, D), jnp.float32), 'gate_w': jax.random.normal(ks[1], (E, D), jnp.float32) * s(D), 'w_gate': jax.random.normal(ks[2], (E, D, H), jnp.float32) * s(D), 'w_up': jax.random.normal(ks[3], (E, D, H), jnp.float32) * s(D), 'w_down': jax.random.normal(ks[4], (E, H, D), jnp.float32) * s(H), 'sw_gate': jax.random.normal(ks[5], (D, H), jnp.float32) * s(D), 'sw_up': jax.random.normal(ks[6], (D, H), jnp.float32) * s(D), 'sw_down': jax.random.normal(ks[7], (H, D), jnp.float32) * s(H)}
    _L1_ffn_all = _L1_ffn_setup()
    _L1_ffn_in = {k: v for k, v in _L1_ffn_all.items() if k in ('gate_w', 'w_gate', 'w_up', 'w_down', 'sw_gate', 'sw_up', 'sw_down')}
    del _L1_ffn_all
    return {'x': x, 'ctx_1024': ctx_1024, 'mask_1x1xSxS2_bk1': mask_1x1xSxS2_bk1, 'L0_xattn_Wq': _L0_xattn_in['Wq'], 'L0_xattn_bq': _L0_xattn_in['bq'], 'L0_xattn_Wk': _L0_xattn_in['Wk'], 'L0_xattn_bk': _L0_xattn_in['bk'], 'L0_xattn_Wv': _L0_xattn_in['Wv'], 'L0_xattn_bv': _L0_xattn_in['bv'], 'L0_xattn_Wo': _L0_xattn_in['Wo'], 'L0_xattn_bo': _L0_xattn_in['bo'], 'L0_xattn_rpe_table': _L0_xattn_in['rpe_table'], 'L0_ffn_U1': _L0_ffn_in['U1'], 'L0_ffn_V1': _L0_ffn_in['V1'], 'L0_ffn_b1': _L0_ffn_in['b1'], 'L0_ffn_U2': _L0_ffn_in['U2'], 'L0_ffn_V2': _L0_ffn_in['V2'], 'L0_ffn_b2': _L0_ffn_in['b2'], 'L1_xattn_Wq': _L1_xattn_in['Wq'], 'L1_xattn_bq': _L1_xattn_in['bq'], 'L1_xattn_Wk': _L1_xattn_in['Wk'], 'L1_xattn_bk': _L1_xattn_in['bk'], 'L1_xattn_Wv': _L1_xattn_in['Wv'], 'L1_xattn_bv': _L1_xattn_in['bv'], 'L1_xattn_Wo': _L1_xattn_in['Wo'], 'L1_xattn_bo': _L1_xattn_in['bo'], 'L1_ffn_gate_w': _L1_ffn_in['gate_w'], 'L1_ffn_w_gate': _L1_ffn_in['w_gate'], 'L1_ffn_w_up': _L1_ffn_in['w_up'], 'L1_ffn_w_down': _L1_ffn_in['w_down'], 'L1_ffn_sw_gate': _L1_ffn_in['sw_gate'], 'L1_ffn_sw_up': _L1_ffn_in['sw_up'], 'L1_ffn_sw_down': _L1_ffn_in['sw_down']}

def reference(x, ctx_1024, mask_1x1xSxS2_bk1, L0_xattn_Wq, L0_xattn_bq, L0_xattn_Wk, L0_xattn_bk, L0_xattn_Wv, L0_xattn_bv, L0_xattn_Wo, L0_xattn_bo, L0_xattn_rpe_table, L0_ffn_U1, L0_ffn_V1, L0_ffn_b1, L0_ffn_U2, L0_ffn_V2, L0_ffn_b2, L1_xattn_Wq, L1_xattn_bq, L1_xattn_Wk, L1_xattn_bk, L1_xattn_Wv, L1_xattn_bv, L1_xattn_Wo, L1_xattn_bo, L1_ffn_gate_w, L1_ffn_w_gate, L1_ffn_w_up, L1_ffn_w_down, L1_ffn_sw_gate, L1_ffn_sw_up, L1_ffn_sw_down):
    import jax
    import jax.numpy as jnp

    def _L0_xattn_ref(query, key, value, mask, Wq, bq, Wk, bk, Wv, bv, Wo, bo, rpe_table):
        import jax, jax.numpy as jnp
        import numpy as np
        import math
        D_MODEL = 128
        NUM_HEADS = 16
        D_K = D_MODEL // NUM_HEADS
        SEQ = 512
        BATCH = 1
        NUM_BUCKETS = 32
        MAX_DISTANCE = 512

        def _relative_position_bucket(relative_position):
            n = jnp.maximum(-relative_position, 0)
            max_exact = NUM_BUCKETS // 2
            is_small = n < max_exact
            nf = jnp.maximum(n, 1).astype(jnp.float32)
            val_if_large = max_exact + (jnp.log(nf / max_exact) / math.log(MAX_DISTANCE / max_exact) * (NUM_BUCKETS - max_exact)).astype(jnp.int32)
            val_if_large = jnp.minimum(val_if_large, NUM_BUCKETS - 1)
            return jnp.where(is_small, n, val_if_large)
        B, S, _ = query.shape
        scale = jnp.sqrt(jnp.asarray(D_K, jnp.float32))

        def heads(x, W, b):
            return (x @ W + b).reshape(B, S, NUM_HEADS, D_K).transpose(0, 2, 1, 3)
        Q = heads(query, Wq, bq)
        K = heads(key, Wk, bk)
        V = heads(value, Wv, bv)
        energy = jnp.einsum('bhqd,bhkd->bhqk', Q, K) / scale
        pos = jnp.arange(S)
        rel = pos[None, :] - pos[:, None]
        bucket = _relative_position_bucket(rel)
        bias = rpe_table[bucket]
        energy = energy + bias.transpose(2, 0, 1)[None]
        neg = jnp.finfo(energy.dtype).min
        energy = jnp.where(mask, neg, energy)
        attn = jax.nn.softmax(energy, axis=-1)
        x = jnp.einsum('bhqk,bhkd->bhqd', attn, V)
        x = x.transpose(0, 2, 1, 3).reshape(B, S, D_MODEL)
        return x @ Wo + bo

    def _L0_ffn_ref(x, U1, V1, b1, U2, V2, b2):
        import jax, jax.numpy as jnp
        import numpy as np
        D_MODEL, D_FF, RANK = (128, 512, 32)
        B, S = (4, 512)
        P = jnp.einsum('bsd,dr->bsr', x, U1)
        H = jax.nn.gelu(jnp.einsum('bsr,rf->bsf', P, V1) + b1)
        Q = jnp.einsum('bsf,fr->bsr', H, U2)
        return jnp.einsum('bsr,rd->bsd', Q, V2) + b2

    def _L1_xattn_ref(Q, K, V, Wq, bq, Wk, bk, Wv, bv, Wo, bo):
        import jax, jax.numpy as jnp
        import numpy as np
        N_HEAD = 16
        D_MODEL = 128
        D_K = D_MODEL // N_HEAD
        q = jnp.einsum('bsd,hdk->bhsk', Q, Wq) + bq[None, :, None, :]
        k = jnp.einsum('bsd,hdk->bhsk', K, Wk) + bk[None, :, None, :]
        v = jnp.einsum('bsd,hdk->bhsk', V, Wv) + bv[None, :, None, :]
        scale = 1.0 / jnp.sqrt(jnp.asarray(q.shape[-1], q.dtype))
        scores = jnp.einsum('bhqk,bhsk->bhqs', q, k) * scale
        attn = jax.nn.softmax(scores, axis=-1)
        ctx = jnp.einsum('bhqs,bhsk->bhqk', attn, v)
        B, H, Sq, dk = ctx.shape
        concat = ctx.transpose(0, 2, 1, 3).reshape(B, Sq, H * dk)
        return concat @ Wo + bo

    def _L1_ffn_ref(x, gate_w, w_gate, w_up, w_down, sw_gate, sw_up, sw_down):
        import jax, jax.numpy as jnp
        import numpy as np
        B, L, D = (4, 128, 128)
        E, H, K = (16, 64, 8)
        EPS = 1e-12

        def _l2norm(v, axis=-1):
            n = jnp.sqrt(jnp.sum(v * v, axis=axis, keepdims=True))
            return v / jnp.maximum(n, EPS)
        if __name__ == '__main__':
            out = reference(**setup_inputs())
            print(out.shape)
        b, l, d = x.shape
        xf = x.reshape(-1, d)
        logits = _l2norm(xf) @ _l2norm(gate_w).T
        scores = jax.nn.sigmoid(logits)
        topk_scores, topk_idx = jax.lax.top_k(scores, K)
        topk_w = topk_scores / jnp.sum(topk_scores, axis=-1, keepdims=True)
        combine = jnp.sum(jax.nn.one_hot(topk_idx, E, dtype=xf.dtype) * topk_w[..., None], axis=1)
        g = jnp.einsum('nd,edh->neh', xf, w_gate)
        u = jnp.einsum('nd,edh->neh', xf, w_up)
        y = jnp.einsum('neh,ehd->ned', jax.nn.silu(g) * u, w_down)
        routed = jnp.einsum('ned,ne->nd', y, combine)
        shared = jax.nn.silu(xf @ sw_gate) * (xf @ sw_up) @ sw_down
        return (routed + shared).reshape(b, l, d)
    x = x + _L0_xattn_ref(_layernorm(x, axis=-1), ctx_1024, ctx_1024, mask_1x1xSxS2_bk1, L0_xattn_Wq, L0_xattn_bq, L0_xattn_Wk, L0_xattn_bk, L0_xattn_Wv, L0_xattn_bv, L0_xattn_Wo, L0_xattn_bo, L0_xattn_rpe_table)
    x = x + _L0_ffn_ref(_layernorm(x, axis=-1), L0_ffn_U1, L0_ffn_V1, L0_ffn_b1, L0_ffn_U2, L0_ffn_V2, L0_ffn_b2)
    x = x + _L1_xattn_ref(_layernorm(x, axis=-1), ctx_1024, ctx_1024, L1_xattn_Wq, L1_xattn_bq, L1_xattn_Wk, L1_xattn_bk, L1_xattn_Wv, L1_xattn_bv, L1_xattn_Wo, L1_xattn_bo)
    x = x + _L1_ffn_ref(_layernorm(x, axis=-1), L1_ffn_gate_w, L1_ffn_w_gate, L1_ffn_w_up, L1_ffn_w_down, L1_ffn_sw_gate, L1_ffn_sw_up, L1_ffn_sw_down)
    return x

_drawn_inputs = setup_inputs


def setup_inputs(seed=0):
    import zlib

    import numpy as np

    out = dict(_drawn_inputs(seed))
    spreads = {'L0_xattn_bq': (0.0, 0.1),
     'L0_xattn_bk': (0.0, 0.1),
     'L0_xattn_bv': (0.0, 0.1),
     'L0_xattn_bo': (0.0, 0.1),
     'L0_ffn_b1': (0.0, 0.8),
     'L0_ffn_b2': (0.0, 0.317),
     'L1_xattn_bq': (0.0, 1.432),
     'L1_xattn_bk': (0.0, 2.0),
     'L1_xattn_bv': (0.0, 0.346),
     'L1_xattn_bo': (0.0, 0.322)}
    factors = {'L0_ffn_U1': 8.0, 'L0_ffn_V1': 8.0, 'L0_ffn_U2': 7.982, 'L0_ffn_V2': 7.765}
    for name, (base, spread) in spreads.items():
        noise = np.random.default_rng([zlib.crc32(name.encode()), seed]).standard_normal(out[name].shape)
        drawn = base * np.exp(spread * noise) if base else spread * noise
        out[name] = jnp.asarray(drawn.astype(out[name].dtype))
    for name, factor in factors.items():
        out[name] = (out[name] * factor).astype(out[name].dtype)
    return out
```

```python
from contextlib import ExitStack

import numpy as np

import concourse.bass as bass
from concourse import mybir

F32 = mybir.dt.float32
BF16 = mybir.dt.bfloat16
U8 = mybir.dt.uint8
ACT = mybir.ActivationFunctionType
ALU = mybir.AluOpType
AX = mybir.AxisListType

BATCH, SEQ, D = 8, 128, 128
HEADS, DK = 16, 8
HALF = HEADS // 2
PAIRS = BATCH // 2
TOK = 2 * SEQ
FF, RANK = 512, 32
FCH = FF // 128
EXPERTS, HID, TOPK = 16, 64, 8
ECH = EXPERTS * HID // 128
BUCKETS, MAX_DISTANCE = 32, 512
REL = 2 * SEQ - 1
NEG = -float(2 ** 100)
LN_EPS, L2_EPS = 1e-5, 1e-12
GELU_C, GELU_A = 0.7978845608028654, 0.044715
SCALE = float(DK) ** -0.5

Q_PART = (0, 0, 0, 1, 1, 2)
K_PART = (0, 1, 2, 0, 1, 0)
PRODS = len(Q_PART)
HROWS = PRODS * DK
SROWS = 2 * HROWS
QROWS = SROWS + 3
VW = 32


def bass_xattn_ffn_moe(nc, x_d, ctx_d, mask_d, wqk_d, wv_d, wo_d, bqk_d, bv_d, rows_d, table_d, u1t_d, v1_d, b1_d,
                       u2t_d, v2_d, gate_d, wg_d, wu_d, wd_d, swd_d, ident_d, onehot_d, expsel_d, out_d):
    rel_d = nc.dram_tensor("rel_bias_scratch", (HEADS, REL + 1), F32, kind="Internal").ap()

    with ExitStack() as ctx:
        def sb(name, shape, dt=F32):
            return ctx.enter_context(nc.sbuf_tensor(name, shape, dt))

        sems = {}

        def sem(name):
            if name not in sems:
                sems[name] = ctx.enter_context(nc.semaphore(name))
            return sems[name]

        def after(eng, name, p, n=None, of=1):
            n = of if n is None else n
            v = p * of + n
            if not (isinstance(v, int) and v <= 0):
                eng.wait_ge(sem(name), v)

        def before(eng, name, p, of=1):
            if not (isinstance(p, int) and p == 0):
                eng.wait_ge(sem(name), p * of)

        bank = [ctx.enter_context(nc.psum_tensor(f"bank{i}", [128, 512], F32)) for i in range(8)]
        S_BANK, T_BANK, C_BANK, M_BANK = bank[0:2], bank[2:4], bank[4:6], bank[6:8]

        FRONT = ["xn0T", "cT", "k", "q0", "v"]
        ATTN = [[f"nmT{l}0", f"nmT{l}1", f"o{l}"] for l in range(2)]
        BEFORE = ATTN[0] + ["xn1T", "ff0", "ff1", "xn2T", "q1"] + ATTN[1]
        MOE = ["xn3T", "logit", "combT", "shared"]
        RINGS = {
            "m": (M_BANK, ["w1", "w2", "rel0", "maskT", "gateT"] + FRONT, BEFORE + FRONT + MOE, BEFORE + MOE),
            "s": (S_BANK, [],) + ([f"S{l}{b}{c}" for l in range(2) for b in range(2) for c in range(4)]
                                  + [f"gu{c}" for c in range(ECH)],) * 2,
            "t": (T_BANK, [],) + ([f"T{l}{b}{c}" for l in range(2) for b in range(2) for c in range(4)]
                                  + [f"cb{c}" for c in range(ECH)],) * 2,
        }

        def number(ring, name, turn):
            _, setup, body, last = RINGS[ring]
            assert len(setup) % 2 == 0 and len(body) % 2 == 0
            if isinstance(turn, str):
                n = setup.index(name)
                return n % 2, n // 2
            uses = last if isinstance(turn, int) and turn == PAIRS - 1 else body
            n = uses.index(name)
            return n % 2, turn * (len(body) // 2) + (len(setup) + n) // 2

        def fill(pe, ring, name, turn):
            k, n = number(ring, name, turn)
            if not (isinstance(n, int) and n == 0):
                pe.wait_ge(sem(f"{ring}_free{k}"), n)
            return RINGS[ring][0][k]

        def filled(ins, ring, name, turn):
            ins.then_inc(sem(f"{ring}_full{number(ring, name, turn)[0]}"), 1)

        def read(eng, ring, name, turn):
            k, n = number(ring, name, turn)
            eng.wait_ge(sem(f"{ring}_full{k}"), n + 1)
            return RINGS[ring][0][k]

        def free(ins, ring, name, turn):
            ins.then_inc(sem(f"{ring}_free{number(ring, name, turn)[0]}"), 1)

        def freed(eng, ring, name, turn):
            k, n = number(ring, name, turn)
            eng.wait_ge(sem(f"{ring}_free{k}"), n + 1)

        wqk = sb("wqk", [128, 2, 2, D])
        wv = sb("wv", [128, 2, D])
        wo = sb("wo", [128, 2, D])
        bqk = sb("bqk", [128, 4])
        bqs = sb("bqs", [128, 2])
        bvb = sb("bvb", [128, 2, 2 * D])
        rowb = sb("rowb", [128, 3, 2, D])
        table = sb("table", [BUCKETS, HEADS])
        onehot = sb("onehot", [BUCKETS, REL + 1])
        u1t = sb("u1t", [RANK, D])
        v1 = sb("v1", [RANK, FF])
        b1 = sb("b1", [128, FCH])
        u2t = sb("u2t", [RANK, FF])
        v2 = sb("v2", [RANK, D])
        w1 = sb("w1", [128, FF])
        w2 = sb("w2", [128, FCH, D])
        gate = sb("gate", [EXPERTS, D])
        gsq = sb("gsq", [EXPERTS, D])
        gss = sb("gss", [EXPERTS, 2])
        gateT = sb("gateT", [128, EXPERTS])
        wg = sb("wg", [128, EXPERTS * HID + HID])
        wu = sb("wu", [128, EXPERTS * HID + HID])
        wd = sb("wd", [128, ECH, D])
        swd = sb("swd", [HID, D])
        ident = sb("ident", [128, 128])
        identb = sb("identb", [128, 128], BF16)
        expself = sb("expself", [3 * EXPERTS, ECH, 128])
        expsel = sb("expsel", [3 * EXPERTS, ECH, 128], BF16)
        mask8 = sb("mask8", [SEQ, SEQ], U8)
        maskn = sb("maskn", [SEQ, SEQ])
        masknT = sb("masknT", [SEQ, SEQ])
        relrow = sb("relrow", [HEADS, REL + 1])
        biasq = sb("biasq", [SEQ, HALF, 2, SEQ])
        biask = sb("biask", [SEQ, HALF, 2, SEQ])
        half = sb("half", [128, 4])

        x0 = sb("x0", [128, 2, D])
        cx = sb("cx", [128, 2, D])
        res = [sb(f"res{n}", [128, 2, D]) for n in range(4)]
        xs = [None] + [sb(f"x{n}", [128, 2, D]) for n in range(1, 4)]
        xout = sb("xout", [128, 2, D])
        xn = [sb(f"xn{n}", [128, 2, D]) for n in range(4)]
        xnT = [sb(f"xnT{n}", [128, TOK]) for n in range(4)]
        cT = sb("cT_sb", [128, TOK])
        stats = sb("stats", [128, 4, 2, 6])
        mv = sb("mv", [128, 4, 2, 2])
        ve = sb("ve", [128, 4, 2])
        rstd = sb("rstd", [128, 4, 2])
        dummy = sb("tiny", [128, 4])
        qf = sb("qf", [128, TOK])
        qr = sb("qr", [128, TOK])
        qsp = sb("qsp", [128, 3, TOK], BF16)
        kf = sb("kf", [128, 2, TOK])
        kr = sb("kr", [128, 2, TOK])
        ksp = sb("ksp", [128, 3, 2, TOK], BF16)
        qz = sb("qz", [QROWS, HALF, 2, TOK], BF16)
        kst = sb("kst", [QROWS, 2, HALF, TOK], BF16)
        va = sb("va", [128, 2, 2, HEADS, VW])
        es = sb("es", [128, 2, 512])
        et = sb("et", [128, 4, 512])
        mx = sb("mx", [128, 2, HEADS])
        mr = sb("mr", [128, 2, HEADS])
        nmw = sb("nm", [128, 2, 128], BF16)
        nm = nmw[:, :, 0:3 * HEADS].rearrange("p b (n h) -> p b n h", n=3)
        nmT = sb("nmT_sb", [3 * HEADS, 2, SEQ], BF16)
        pt = sb("pt", [128, 2, HEADS, SEQ])
        ct1 = sb("ct1", [128, 2, 4, 4, 32])
        crc = sb("crc", [128, 2, 4, 4])
        ct2 = sb("ct2", [128, 2, 4, 4, DK])
        ct3 = sb("ct3", [128, 2, SEQ])
        fv = sb("fv", [128, FCH, TOK])
        fs = sb("fs", [128, FCH, TOK])
        fw = sb("fw", [128, FCH, TOK])
        fh = sb("fh", [128, FCH, TOK])
        sq = sb("sq", [128, 2, D])
        ss = sb("ss", [128, 2])
        sc = sb("sc", [128, 2])
        rn = sb("rn", [128, 2])
        lg = sb("lg", [128, 2, EXPERTS])
        top = sb("top", [128, 2, TOPK])
        lr = sb("lr", [128, 2, EXPERTS])
        sel = sb("sel", [128, 2, EXPERTS])
        th = sb("th", [128, 2, EXPERTS])
        sw = sb("sw", [128, 2, EXPERTS])
        sws = sb("sws", [128, 2])
        swr = sb("swr", [128, 2])
        comb = sb("comb", [128, 2, EXPERTS])
        cr = sb("cr", [128, 2, EXPERTS])
        cspw = sb("csp", [128, 2, 128], BF16)
        csp = cspw[:, :, 0:3 * EXPERTS].rearrange("p b (n e) -> p b n e", n=3)
        combT = sb("combT_sb", [3 * EXPERTS, TOK], BF16)
        gth = sb("gth", [128, 2, TOK])
        ga = sb("ga", [128, 2, TOK])
        gb = sb("gb", [128, 2, TOK])
        hT = sb("hT", [128, 2, TOK])

        block = ctx.enter_context(nc.Block())

        @block.sync
        def _(sp):
            def load_pair(p):
                sp.dma_start(x0[:], x_d[bass.ds(2 * p, 2)].rearrange("b s d -> s b d")).then_inc(sem("x0_in"), 16)
                sp.dma_start(cx[:], ctx_d[bass.ds(2 * p, 2)].rearrange("b s d -> s b d")).then_inc(sem("cx_in"), 16)

            def stack_q(l, p, turn):
                after(sp, f"q_split", 2 * p + l)
                for hh in range(2):
                    for n, part in enumerate(Q_PART):
                        r = HROWS * hh + DK * n
                        sp.dma_start(qz[r:r + DK, :, hh, :],
                                     qsp[64 * hh:64 * hh + 64, part, :]).then_inc(sem("qz_in"), 16)

            def stack_k(p, turn):
                after(sp, "k_split", p)
                for hh in range(2):
                    for n, part in enumerate(K_PART):
                        for l in range(2):
                            r = HROWS * hh + DK * n
                            sp.dma_start(kst[r:r + DK, l, :, :],
                                         ksp[64 * hh:64 * hh + 64, part, l, :]).then_inc(sem("kst_in"), 16)

            def max_rows(l, p):
                for b in range(2):
                    freed(sp, "m", f"nmT{l}{b}", p)
                    sp.dma_start(qz[SROWS:QROWS, :, :, b * SEQ:(b + 1) * SEQ],
                                 nmT[:, b, :]).then_inc(sem(f"max_in{b}"), 16)

            sp.dma_start(ident[:], ident_d).then_inc(sem("ident_in"), 16)
            load_pair(0)
            sp.dma_start(wqk[:], wqk_d).then_inc(sem("proj_in"), 16)
            sp.dma_start(wv[:], wv_d).then_inc(sem("proj_in"), 16)
            sp.dma_start(bqk[:], bqk_d).then_inc(sem("bqk_in"), 16)
            sp.dma_start(bvb[:], bv_d.partition_broadcast(128)).then_inc(sem("bias_in"), 16)
            sp.dma_start(rowb[:], rows_d.partition_broadcast(128)).then_inc(sem("bias_in"), 16)
            sp.dma_start(table[:], table_d).then_inc(sem("rel_in"), 16)
            sp.dma_start(onehot[:], onehot_d).then_inc(sem("rel_in"), 16)
            sp.dma_start(mask8[:], mask_d).then_inc(sem("mask_in"), 16)
            sp.dma_start(u1t[:], u1t_d).then_inc(sem("ffw_in"), 16)
            sp.dma_start(v1[:], v1_d).then_inc(sem("ffw_in"), 16)
            sp.dma_start(u2t[:], u2t_d).then_inc(sem("ffw_in"), 16)
            sp.dma_start(v2[:], v2_d).then_inc(sem("ffw_in"), 16)
            sp.dma_start(b1[:], b1_d).then_inc(sem("b1_in"), 16)
            sp.dma_start(gate[:], gate_d).then_inc(sem("gate_in"), 16)
            sp.dma_start(expself[:], expsel_d).then_inc(sem("expsel_in"), 16)
            freed(sp, "m", "rel0", "setup")
            sp.dma_start(rel_d, relrow[:]).then_inc(sem("rel_out"), 16)
            sp.wait_ge(sem("rel_out"), 16)
            rel_t = rel_d.tensor
            for tile in (biasq, biask):
                for hh in range(2):
                    src = bass.AP(tensor=rel_t, offset=HALF * hh * (REL + 1),
                                  ap=[[1, SEQ], [REL + 1, HALF], [1, SEQ]])
                    sp.dma_start(tile[:, :, hh, :], src).then_inc(sem("biasqk_in"), 16)
            sp.wait_ge(sem("stacks_cleared"), 2)
            stack_k(0, "setup")
            stack_q(0, 0, "setup")
            sp.dma_start(wo[:], wo_d).then_inc(sem("late_in"), 16)
            sp.dma_start(wg[:], wg_d).then_inc(sem("late_in"), 16)
            sp.dma_start(wu[:], wu_d).then_inc(sem("late_in"), 16)
            sp.dma_start(wd[:], wd_d).then_inc(sem("late_in"), 16)
            sp.dma_start(swd[:], swd_d).then_inc(sem("late_in"), 16)

            def body(i, last):
                first = 2 * i if isinstance(i, int) else sp.snap(2 * i)
                if not last:
                    load_pair(i + 1)
                max_rows(0, i)
                stack_q(1, i, i)
                max_rows(1, i)
                if not last:
                    stack_k(i + 1, i)
                    stack_q(0, i + 1, i)
                after(sp, "xout", i, of=2)
                sp.dma_start(out_d[bass.ds(first, 2)].rearrange("b s d -> s b d"), xout[:]).then_inc(sem("stored"), 16)

            body(0, False)
            with sp.Fori(1, PAIRS - 1) as i:
                body(i, False)
            body(PAIRS - 1, True)
            sp.wait_ge(sem("stored"), 16 * PAIRS)

        @block.gpsimd
        def _(pool):
            pool.memset(half[:], -0.5).then_inc(sem("half"), 1)
            pool.memset(qz[:], 0.0).then_inc(sem("stacks_cleared"), 1)
            pool.memset(kst[:], 0.0).then_inc(sem("kst_cleared"), 1)
            pool.wait_ge(sem("kst_cleared"), 1)
            pool.memset(kst[SROWS:QROWS], 1.0).then_inc(sem("stacks_cleared"), 1)
            pool.wait_ge(sem("stacks_cleared"), 2)
            pool.memset(va[:], 0.0).then_inc(sem("va_cleared"), 1)
            pool.wait_ge(sem("va_cleared"), 1)
            pool.memset(va[:, :, :, :, DK:DK + 1], 1.0).then_inc(sem("va_ones"), 1)
            pool.wait_ge(sem("half"), 1)

            def power(n, p):
                after(pool, f"ve{n}", p)
                pool.tensor_tensor(rstd[:, n, :], ve[:, n, :], half[:, 0:2], ALU.pow).then_inc(sem(f"rstd{n}"), 1)

            def residual(n, src, came):
                came()
                pool.tensor_tensor(res[n][:], src[:], rowb[:, n], ALU.add).then_inc(sem(f"res{n}"), 1)

            def split_q(l, p, turn):
                freed(pool, "m", f"q{l}", turn)
                pool.tensor_tensor(qr[:], qf[:], qsp[:, 0], ALU.subtract).then_inc(sem("q_rest"), 1)
                after(pool, "q_mid", 2 * p + l)
                pool.tensor_tensor(qsp[:, 2], qr[:], qsp[:, 1], ALU.subtract).then_inc(sem("q_split"), 1)

            def front(p, turn):
                power(0, p)
                if not isinstance(turn, str):
                    freed(pool, "m", "o0", turn)
                residual(0, x0, lambda: after(pool, "x0_in", p, of=16))
                freed(pool, "m", "k", turn)
                pool.tensor_tensor(kr[:], kf[:], ksp[:, 0], ALU.subtract).then_inc(sem("k_rest"), 1)
                after(pool, "k_mid", p)
                pool.tensor_tensor(ksp[:, 2], kr[:], ksp[:, 1], ALU.subtract).then_inc(sem("k_split"), 1)
                split_q(0, p, turn)

            pool.wait_ge(sem("gss"), 1)
            pool.tensor_tensor(gss[:, 1:2], gss[:, 0:1], half[0:EXPERTS, 0:1], ALU.pow).then_inc(sem("gate_norm"), 1)
            pool.wait_ge(sem("bias_in"), 32)
            front(0, "setup")

            def body(i, last):
                residual(1, xs[1], lambda: freed(pool, "m", "o0", i))
                power(1, i)
                residual(2, xs[2], lambda: after(pool, "x2", i, of=2))
                power(2, i)
                split_q(1, i, i)
                power(3, i)
                if not last:
                    front(i + 1, i)
                after(pool, "ss_clamped", i)
                pool.tensor_tensor(rn[:], sc[:], half[:, 0:2], ALU.pow).then_inc(sem("rn"), 1)

            body(0, False)
            with pool.Fori(1, PAIRS - 1) as i:
                body(i, False)
            body(PAIRS - 1, True)

        @block.scalar
        def _(act):
            def project_q(l, p, turn):
                src = read(act, "m", f"q{l}", turn)[:, 0:TOK]
                n = 2 * p + l
                before(act, "qz_in", n, of=2 * PRODS * 16)
                act.activation(qf[:], src, ACT.Identity, bias=bqs[:, l:l + 1], scale=SCALE)
                free(act.activation(qsp[:, 0], src, ACT.Identity, bias=bqs[:, l:l + 1], scale=SCALE),
                     "m", f"q{l}", turn)
                after(act, "q_rest", n)
                act.activation(qsp[:, 1], qr[:], ACT.Copy).then_inc(sem("q_mid"), 1)

            def front(p, turn):
                src = read(act, "m", "cT", turn)[:, 0:TOK]
                free(act.activation(cT[:], src, ACT.Copy), "m", "cT", turn)
                src = read(act, "m", "xn0T", turn)[:, 0:TOK]
                free(act.activation(xnT[0][:], src, ACT.Copy), "m", "xn0T", turn)
                src = read(act, "m", "k", turn)
                before(act, "kst_in", p, of=4 * PRODS * 16)
                for l in range(2):
                    for dst in (kf[:, l], ksp[:, 0, l]):
                        ins = act.activation(dst, src[:, l * TOK:(l + 1) * TOK], ACT.Identity,
                                             bias=bqk[:, 2 * l + 1:2 * l + 2])
                free(ins, "m", "k", turn)
                after(act, "k_rest", p)
                act.activation(ksp[:, 1], kr[:], ACT.Copy).then_inc(sem("k_mid"), 1)
                project_q(0, p, turn)

            def max_turned(l, i):
                for b in range(2):
                    src = read(act, "m", f"nmT{l}{b}", i)
                    v = src[:].bitcast(BF16)[0:3 * HEADS, 0:SEQ]
                    if l:
                        after(act, f"max_in{b}", i, 16, 32)
                    else:
                        before(act, f"max_in{b}", i, of=32)
                    free(act.activation(nmT[:, b], v, ACT.Copy), "m", f"nmT{l}{b}", i)

            def softmax(l, i):
                for b in range(2):
                    if l:
                        after(act, f"pv0{b}", i)
                    else:
                        before(act, f"pv1{b}", i)
                    for c in range(4):
                        dst = pt[:, b, 4 * c:4 * c + 4, :]
                        if l == 0:
                            freed(act, "t", f"T0{b}{c}", i)
                            ins = act.activation(dst, et[:, c, :], ACT.Exp)
                            ins.then_inc(sem(f"p0{b}"), 1)
                        else:
                            src = read(act, "t", f"T1{b}{c}", i)
                            free(act.activation(dst, src[:], ACT.Exp), "t", f"T1{b}{c}", i)

            act.wait_ge(sem("bqk_in"), 16)
            act.activation(bqs[:], bqk[:].rearrange("p (l n) -> p n l", n=2)[:, 0, :], ACT.Copy, scale=SCALE)\
               .then_inc(sem("bqs"), 1)
            act.wait_ge(sem("gate_in"), 16)
            act.activation(gsq[:], gate[:], ACT.Square, accum_out=gss[:, 0:1]).then_inc(sem("gsq"), 1)
            act.wait_ge(sem("half"), 1)
            act.wait_ge(sem("bqs"), 1)
            front(0, "setup")

            def body(i, last):
                max_turned(0, i)
                softmax(0, i)
                src = read(act, "m", "xn1T", i)[:, 0:TOK]
                free(act.activation(xnT[1][:], src, ACT.Copy), "m", "xn1T", i)
                act.wait_ge(sem("b1_in"), 16)
                for n in range(FCH // 2):
                    src = read(act, "m", f"ff{n}", i)
                    for k in range(2):
                        f = 2 * n + k
                        act.activation(fv[:, f], src[:, k * TOK:(k + 1) * TOK], ACT.Identity,
                                       bias=b1[:, f:f + 1]).then_inc(sem("fv"), 1)
                    after(act, "fv", i, 2 * n + 2, FCH)
                    ins = act.activation(fs[:, 2 * n:2 * n + 2], fv[:, 2 * n:2 * n + 2], ACT.Square)
                    free(ins, "m", f"ff{n}", i)
                for n in range(2):
                    after(act, "fw", i, n + 1, 2)
                    act.activation(fs[:, 2 * n:2 * n + 2], fw[:, 2 * n:2 * n + 2], ACT.Tanh, scale=GELU_C)\
                       .then_inc(sem("ftanh"), 1)
                src = read(act, "m", "xn2T", i)[:, 0:TOK]
                free(act.activation(xnT[2][:], src, ACT.Copy), "m", "xn2T", i)
                project_q(1, i, i)
                max_turned(1, i)
                softmax(1, i)
                if not last:
                    front(i + 1, i)
                after(act, "xn3", i, of=2)
                for b in range(2):
                    act.activation(sq[:, b], xn[3][:, b], ACT.Square, accum_out=ss[:, b:b + 1]).then_inc(sem("ss"), 1)
                src = read(act, "m", "xn3T", i)[:, 0:TOK]
                free(act.activation(xnT[3][:], src, ACT.Copy), "m", "xn3T", i)
                freed(act, "m", "logit", i)
                act.activation(th[:], lg[:], ACT.Tanh, scale=0.5).then_inc(sem("th"), 1)
                src = read(act, "m", "combT", i)
                v = src[:].bitcast(BF16)[0:3 * EXPERTS, 0:TOK]
                free(act.activation(combT[:], v, ACT.Copy), "m", "combT", i)
                for c in range(ECH + 1):
                    if c >= 2:
                        after(act, "ga", i, c - 1, ECH + 1)
                    else:
                        before(act, "ga", i, of=ECH + 1)
                    if c < ECH:
                        src, rows = read(act, "s", f"gu{c}", i), 128
                    else:
                        src, rows = read(act, "m", "shared", i), HID
                    act.activation(gth[0:rows, c % 2], src[0:rows, 0:TOK], ACT.Tanh, scale=0.5).then_inc(sem("gth"), 1)

            body(0, False)
            with act.Fori(1, PAIRS - 1) as i:
                body(i, False)
            body(PAIRS - 1, True)

        @block.vector
        def _(dve):
            def norm(n, src, p):
                for b in range(2):
                    dve.bn_stats(stats[:, n, b], src[:, b]).then_inc(sem(f"stats{n}"), 1)
                after(dve, f"stats{n}", p, of=2)
                dve.tensor_copy(dummy[:, 1:2], half[:, 0:1]).then_inc(sem("wait_carried"), 1)
                for b in range(2):
                    dve.bn_aggr(mv[:, n, b], stats[:, n, b]).then_inc(sem(f"mv{n}"), 1)
                after(dve, f"mv{n}", p, of=2)
                dve.tensor_scalar(ve[:, n], mv[:, n, :, 1], LN_EPS, None, ALU.add).then_inc(sem(f"ve{n}"), 1)
                after(dve, f"rstd{n}", p)
                for b in range(2):
                    dve.tensor_scalar(xn[n][:, b], src[:, b], mv[:, n, b, 0:1], rstd[:, n, b:b + 1],
                                      ALU.subtract, ALU.mult).then_inc(sem(f"xn{n}"), 1)

            def front(p, turn):
                after(dve, "x0_in", p, of=16)
                norm(0, x0, p)
                src = read(dve, "m", "v", turn)
                before(dve, "pv11", p)
                ins = dve.tensor_tensor(va[:, :, :, :, 0:DK].rearrange("p b l h d -> p (b l h) d"),
                                        src[:].rearrange("p (n d) -> p n d", d=DK),
                                        bvb[:].rearrange("p b (n d) -> p (b n) d", d=DK), ALU.add)
                free(ins, "m", "v", turn)

            def row_max(l, b, i):
                for c in range(4):
                    src = read(dve, "s", f"S{l}{b}{c}", i)
                    if l == 0:
                        free(dve.tensor_tensor(es[:, c % 2], src[:], biasq[:, 2 * c:2 * c + 2], ALU.add),
                             "s", f"S{l}{b}{c}", i)
                        freed(dve, "s", f"S{l}{b}{c}", i)
                        src = es[:, c % 2]
                        ins = dve.tensor_reduce(mx[:, b, 4 * c:4 * c + 4], src.rearrange("p (h k) -> p h k", h=4),
                                                AX.X, ALU.max)
                        ins.then_inc(sem(f"mx0{b}"), 1)
                        after(dve, f"mx0{b}", i, c + 1, 4)
                    else:
                        ins = dve.tensor_reduce(mx[:, b, 4 * c:4 * c + 4], src[:].rearrange("p (h k) -> p h k", h=4),
                                                AX.X, ALU.max)
                        free(ins, "s", f"S{l}{b}{c}", i)
                        freed(dve, "s", f"S{l}{b}{c}", i)
                dve.tensor_scalar(nm[:, b, 0], mx[:, b], -1.0, None, ALU.mult).then_inc(sem("nm_a"), 1)
                after(dve, "nm_a", i, 2 * l + b + 1, 4)
                dve.scalar_tensor_tensor(mr[:, b], mx[:, b], -1.0, nm[:, b, 0], ALU.mult, ALU.subtract)\
                   .then_inc(sem("nm_b"), 1)
                after(dve, "nm_b", i, 2 * l + b + 1, 4)
                dve.tensor_copy(nm[:, b, 1], mr[:, b]).then_inc(sem("nm_c"), 1)
                after(dve, "nm_c", i, 2 * l + b + 1, 4)
                dve.tensor_tensor(nm[:, b, 2], mr[:, b], nm[:, b, 1], ALU.subtract).then_inc(sem(f"nm{l}{b}"), 1)

            def add_bias(b, i):
                for c in range(4):
                    src = read(dve, "t", f"T0{b}{c}", i)
                    if b:
                        after(dve, "p00", i, c + 1, 4)
                    else:
                        before(dve, "p01", i, of=4)
                    free(dve.tensor_tensor(et[:, c], src[:], biask[:, 2 * c:2 * c + 2], ALU.add),
                         "t", f"T0{b}{c}", i)

            def context(l, b, i):
                after(dve, f"pv{l}{b}", i)
                dve.transpose(ct1[:, b], C_BANK[b][:]).then_inc(sem(f"c_read{l}{b}"), 1)
                after(dve, f"c_read{l}{b}", i)
                dve.reciprocal(crc[:, b], ct1[:, b, :, :, DK]).then_inc(sem("crc"), 1)
                after(dve, "crc", i, 2 * l + b + 1, 4)
                dve.tensor_tensor(ct2[:, b].rearrange("p q g d -> p g q d"), ct1[:, b, :, :, 0:DK],
                                  crc[:, b].unsqueeze(3).broadcast_to([128, 4, 4, DK]), ALU.mult)\
                   .then_inc(sem("ct2"), 1)
                after(dve, "ct2", i, 2 * l + b + 1, 4)
                dve.transpose(ct3[:, b], ct2[:, b]).then_inc(sem(f"ct3{l}"), 1)

            def add_residual(l, i):
                src = read(dve, "m", f"o{l}", i)
                n = 1 if l == 0 else 3
                after(dve, "res0" if l == 0 else "res2", i)
                dst = xs[n]
                free(dve.tensor_tensor(dst[:], src[:, 0:TOK].rearrange("p (b d) -> p b d", b=2), res[n - 1][:],
                                       ALU.add), "m", f"o{l}", i)
                freed(dve, "m", f"o{l}", i)

            dve.wait_ge(sem("half"), 1)
            dve.memset(nmw[:], 0.0).then_inc(sem("pads"), 1)
            dve.memset(cspw[:], 0.0).then_inc(sem("pads"), 1)
            dve.wait_ge(sem("ident_in"), 16)
            dve.tensor_copy(identb[:], ident[:]).then_inc(sem("identb"), 1)
            dve.wait_ge(sem("gsq"), 1)
            dve.tensor_scalar(gss[:, 0:1], gss[:, 0:1], L2_EPS * L2_EPS, None, ALU.max).then_inc(sem("gss"), 1)
            dve.wait_ge(sem("gate_norm"), 1)
            dve.tensor_scalar(gsq[:], gate[:], gss[:, 1:2], None, ALU.mult).then_inc(sem("gate_normed"), 1)
            dve.wait_ge(sem("mask_in"), 16)
            dve.tensor_scalar(maskn[:], mask8[:], NEG, None, ALU.mult).then_inc(sem("maskn"), 1)
            dve.wait_ge(sem("expsel_in"), 16)
            dve.tensor_copy(expsel[:], expself[:]).then_inc(sem("expsel"), 1)
            free(dve.tensor_copy(w1[:], read(dve, "m", "w1", "setup")[:]), "m", "w1", "setup")
            free(dve.tensor_scalar(w2[:], read(dve, "m", "w2", "setup")[:].rearrange("p (n d) -> p n d", n=FCH),
                                   0.5, None, ALU.mult), "m", "w2", "setup")
            src = read(dve, "m", "rel0", "setup")
            free(dve.tensor_copy(relrow[:], src[0:HEADS, 0:REL + 1]), "m", "rel0", "setup")
            free(dve.tensor_copy(masknT[:], read(dve, "m", "maskT", "setup")[:, 0:SEQ]), "m", "maskT", "setup")
            free(dve.tensor_copy(gateT[:], read(dve, "m", "gateT", "setup")[:, 0:EXPERTS]), "m", "gateT", "setup")
            dve.wait_ge(sem("bias_in"), 32)
            dve.wait_ge(sem("va_ones"), 1)
            dve.wait_ge(sem("pads"), 2)
            front(0, "setup")
            dve.wait_ge(sem("biasqk_in"), 64)
            freed(dve, "m", "maskT", "setup")
            for tile, m in ((biasq, maskn), (biask, masknT)):
                v = tile[:].rearrange("p a b k -> p (a b) k")
                dve.tensor_tensor(v, v, m[:].unsqueeze(1).broadcast_to([SEQ, HEADS, SEQ]), ALU.add)\
                   .then_inc(sem("masked"), 1)
            dve.wait_ge(sem("masked"), 2)

            def body(i, last):
                row_max(0, 0, i)
                row_max(0, 1, i)
                add_bias(0, i)
                add_bias(1, i)
                context(0, 0, i)
                context(0, 1, i)
                add_residual(0, i)
                norm(1, xs[1], i)
                for n in range(2):
                    freed(dve, "m", f"ff{n}", i)
                    h = slice(2 * n, 2 * n + 2)
                    dve.tensor_scalar(fw[:, h], fs[:, h], GELU_A, 1.0, ALU.mult, ALU.add).then_inc(sem("fw_a"), 1)
                    after(dve, "fw_a", i, n + 1, 2)
                    dve.tensor_tensor(fw[:, h], fw[:, h], fv[:, h], ALU.mult).then_inc(sem("fw"), 1)
                for n in range(2):
                    after(dve, "ftanh", i, n + 1, 2)
                    h = slice(2 * n, 2 * n + 2)
                    dve.scalar_tensor_tensor(fh[:, h], fs[:, h], 1.0, fv[:, h], ALU.add, ALU.mult).then_inc(sem("fh"), 1)
                after(dve, "res1", i)
                for b in range(2):
                    after(dve, "ffy", i, b + 1, 2)
                    dve.tensor_tensor(xs[2][:, b], C_BANK[b][:, 0:D], res[1][:, b], ALU.add).then_inc(sem("x2"), 1)
                after(dve, "x2", i, of=2)
                norm(2, xs[2], i)
                row_max(1, 0, i)
                row_max(1, 1, i)
                context(1, 0, i)
                context(1, 1, i)
                add_residual(1, i)
                norm(3, xs[3], i)
                if not last:
                    front(i + 1, i)
                after(dve, "ss", i, of=2)
                dve.tensor_scalar(sc[:], ss[:], L2_EPS * L2_EPS, None, ALU.max).then_inc(sem("ss_clamped"), 1)
                src = read(dve, "m", "logit", i)
                after(dve, "rn", i)
                for b in range(2):
                    ins = dve.tensor_scalar(lg[:, b], src[:, b * EXPERTS:(b + 1) * EXPERTS], rn[:, b:b + 1], None, ALU.mult)
                free(ins, "m", "logit", i)
                freed(dve, "m", "logit", i)
                dve.tensor_copy(dummy[:, 2:3], half[:, 0:1]).then_inc(sem("wait_carried"), 1)
                for b in range(2):
                    dve.max(top[:, b], lg[:, b]).then_inc(sem("top"), 1)
                after(dve, "top", i, of=2)
                dve.tensor_copy(dummy[:, 3:4], half[:, 0:1]).then_inc(sem("wait_carried"), 1)
                for b in range(2):
                    dve.match_replace(lr[:, b], top[:, b], lg[:, b], -1e30).then_inc(sem("lr"), 1)
                after(dve, "lr", i, of=2)
                dve.tensor_tensor(sel[:], lr[:], lg[:], ALU.not_equal).then_inc(sem("sel"), 1)
                after(dve, "sel", i)
                after(dve, "th", i)
                dve.scalar_tensor_tensor(sw[:], th[:], 1.0, sel[:], ALU.add, ALU.mult).then_inc(sem("sw"), 1)
                after(dve, "sw", i)
                dve.tensor_reduce(sws[:], sw[:], AX.X, ALU.add).then_inc(sem("sws"), 1)
                after(dve, "sws", i)
                dve.reciprocal(swr[:], sws[:]).then_inc(sem("swr"), 1)
                after(dve, "swr", i)
                for b in range(2):
                    dve.tensor_scalar(comb[:, b], sw[:, b], swr[:, b:b + 1], 0.5, ALU.mult, ALU.mult)\
                       .then_inc(sem("comb"), 1)
                after(dve, "comb", i, of=2)
                dve.tensor_copy(csp[:, :, 0], comb[:]).then_inc(sem("csp"), 1)
                after(dve, "csp", i, 1, 3)
                dve.tensor_tensor(cr[:], comb[:], csp[:, :, 0], ALU.subtract).then_inc(sem("cr"), 1)
                after(dve, "cr", i)
                dve.tensor_copy(csp[:, :, 1], cr[:]).then_inc(sem("csp"), 1)
                after(dve, "csp", i, 2, 3)
                dve.tensor_tensor(csp[:, :, 2], cr[:], csp[:, :, 1], ALU.subtract).then_inc(sem("csp"), 1)
                for c in range(ECH + 1):
                    rows = 128 if c < ECH else HID
                    k = c % 2
                    after(dve, "gth", i, c + 1, ECH + 1)
                    src = read(dve, "s", f"gu{c}", i) if c < ECH else read(dve, "m", "shared", i)
                    dve.scalar_tensor_tensor(ga[0:rows, k], gth[0:rows, k], 1.0, src[0:rows, 0:TOK], ALU.add, ALU.mult)\
                       .then_inc(sem("ga"), 1)
                    after(dve, "ga", i, c + 1, ECH + 1)
                    if c >= 2:
                        after(dve, "down", i, c - 1, ECH + 1)
                    else:
                        before(dve, "down", i, of=ECH + 1)
                    if c < ECH:
                        ins = dve.tensor_tensor(gb[:, k], ga[:, k], src[:, TOK:2 * TOK], ALU.mult)
                        free(ins, "s", f"gu{c}", i)
                        freed(dve, "s", f"gu{c}", i)
                        src = read(dve, "t", f"cb{c}", i)
                        free(dve.tensor_tensor(hT[:, k], gb[:, k], src[:, 0:TOK], ALU.mult), "t", f"cb{c}", i)
                    else:
                        ins = dve.scalar_tensor_tensor(hT[0:rows, k], ga[0:rows, k], 0.5, src[0:rows, TOK:2 * TOK],
                                                       ALU.mult, ALU.mult)
                        free(ins, "m", "shared", i)
                before(dve, "stored", i, of=16)
                after(dve, "down", i, of=ECH + 1)
                for b in range(2):
                    dve.tensor_tensor(xout[:, b], C_BANK[b][:, 0:D], xs[3][:, b], ALU.add).then_inc(sem("xout"), 1)

            body(0, False)
            with dve.Fori(1, PAIRS - 1) as i:
                body(i, False)
            body(PAIRS - 1, True)

        @block.tensor
        def _(pe):
            def turn_tokens(name, src, came, p, turn, of):
                after(pe, came, p, of=of)
                dst = fill(pe, "m", name, turn)
                for b in range(2):
                    ins = pe.transpose(dst[:, b * SEQ:(b + 1) * SEQ], src[:, b], ident[:])
                filled(ins, "m", name, turn)

            def project_q(l, turn):
                freed(pe, "m", f"xn{2 * l}T", turn)
                dst = fill(pe, "m", f"q{l}", turn)
                ins = pe.matmul(dst[:, 0:TOK], wqk[:, l, 0], xnT[2 * l][:], start=True, stop=True)
                filled(ins, "m", f"q{l}", turn)

            def front(p, turn):
                turn_tokens("xn0T", xn[0], "xn0", p, turn, 2)
                turn_tokens("cT", cx, "cx_in", p, turn, 16)
                freed(pe, "m", "cT", turn)
                dst = fill(pe, "m", "k", turn)
                for l in range(2):
                    ins = pe.matmul(dst[:, l * TOK:(l + 1) * TOK], wqk[:, l, 1], cT[:], start=True, stop=True)
                filled(ins, "m", "k", turn)
                project_q(0, turn)
                dst = fill(pe, "m", "v", turn)
                for b in range(2):
                    ins = pe.matmul(dst[:, b * TOK:(b + 1) * TOK], cT[:, b * SEQ:(b + 1) * SEQ], wv[:], start=True, stop=True)
                filled(ins, "m", "v", turn)

            def scores(l, b, i):
                for c in range(4):
                    dst = fill(pe, "s", f"S{l}{b}{c}", i)
                    for s in range(4):
                        hp, hh = (4 * c + s) // 2, (4 * c + s) % 2
                        tok = slice(b * SEQ, (b + 1) * SEQ)
                        ins = pe.matmul(dst[:, s * SEQ:(s + 1) * SEQ], qz[0:SROWS, hp, hh, tok],
                                        kst[0:SROWS, l, hp, tok], start=True, stop=True)
                    filled(ins, "s", f"S{l}{b}{c}", i)

            def turn_max(l, b, i):
                after(pe, f"nm{l}{b}", i)
                dst = fill(pe, "m", f"nmT{l}{b}", i)
                ins = pe.transpose(dst[:].bitcast(BF16)[:, 0:SEQ], nmw[:, b], identb[:])
                filled(ins, "m", f"nmT{l}{b}", i)

            def scores_turned(l, b, i):
                after(pe, f"max_in{b}", i, 16 * (l + 1), 32)
                for c in range(4):
                    dst = fill(pe, "t", f"T{l}{b}{c}", i)
                    tok = slice(b * SEQ, (b + 1) * SEQ)
                    for s in range(2):
                        hp = 2 * c + s
                        ins = pe.matmul(dst[:, 2 * s * SEQ:(2 * s + 2) * SEQ].rearrange("p (h q) -> p h q", h=2),
                                        kst[:, l, hp, tok], qz[:, hp, :, tok], start=True, stop=True)
                    filled(ins, "t", f"T{l}{b}{c}", i)

            def values(l, b, i):
                if l:
                    after(pe, "x2", i, b + 1, 2)
                else:
                    before(pe, "xout", i, of=2)
                for c in range(4):
                    if l:
                        freed(pe, "t", f"T1{b}{c}", i)
                    else:
                        after(pe, f"p0{b}", i, c + 1, 4)
                    for s in range(4 * c, 4 * c + 4):
                        head = HALF * (s % 2) + s // 2
                        j, g = head // 4, head % 4
                        ins = pe.matmul(C_BANK[b][32 * j:32 * j + VW, g * SEQ:(g + 1) * SEQ], va[:, b, l, head],
                                        pt[:, b, s], start=True, stop=True)
                ins.then_inc(sem(f"pv{l}{b}"), 1)

            def attention(l, i):
                after(pe, "kst_in", i, of=4 * PRODS * 16)
                after(pe, "qz_in", 2 * i + l, of=2 * PRODS * 16)
                scores(l, 0, i)
                scores(l, 1, i)
                turn_max(l, 0, i)
                turn_max(l, 1, i)
                for b in range(2):
                    scores_turned(l, b, i)
                for b in range(2):
                    values(l, b, i)
                after(pe, f"ct3{l}", i, of=2)
                dst = fill(pe, "m", f"o{l}", i)
                for b in range(2):
                    ins = pe.matmul(dst[:, b * D:(b + 1) * D], ct3[:, b], wo[:, l], start=True, stop=True)
                filled(ins, "m", f"o{l}", i)

            pe.wait_ge(sem("ffw_in"), 64)
            dst = fill(pe, "m", "w1", "setup")
            filled(pe.matmul(dst[:], u1t[:], v1[:], start=True, stop=True), "m", "w1", "setup")
            dst = fill(pe, "m", "w2", "setup")
            for n in range(FCH):
                ins = pe.matmul(dst[:, n * D:(n + 1) * D], u2t[:, n * 128:(n + 1) * 128], v2[:], start=True, stop=True)
            filled(ins, "m", "w2", "setup")
            pe.wait_ge(sem("rel_in"), 32)
            dst = fill(pe, "m", "rel0", "setup")
            ins = pe.matmul(dst[0:HEADS, 0:REL + 1], table[:], onehot[:], start=True, stop=True)
            filled(ins, "m", "rel0", "setup")
            pe.wait_ge(sem("ident_in"), 16)
            pe.wait_ge(sem("maskn"), 1)
            dst = fill(pe, "m", "maskT", "setup")
            filled(pe.transpose(dst[:, 0:SEQ], maskn[:], ident[:]), "m", "maskT", "setup")
            pe.wait_ge(sem("gate_normed"), 1)
            dst = fill(pe, "m", "gateT", "setup")
            filled(pe.transpose(dst[:, 0:EXPERTS], gsq[:], ident[0:EXPERTS, 0:EXPERTS]), "m", "gateT", "setup")
            pe.wait_ge(sem("proj_in"), 32)
            front(0, "setup")
            pe.wait_ge(sem("identb"), 1)
            pe.wait_ge(sem("late_in"), 80)
            pe.wait_ge(sem("expsel"), 1)

            def body(i, last):
                attention(0, i)
                turn_tokens("xn1T", xn[1], "xn1", i, i, 2)
                freed(pe, "m", "xn1T", i)
                for n in range(FCH // 2):
                    dst = fill(pe, "m", f"ff{n}", i)
                    for k in range(2):
                        f = 2 * n + k
                        ins = pe.matmul(dst[:, k * TOK:(k + 1) * TOK], w1[:, f * 128:(f + 1) * 128], xnT[1][:],
                                        start=True, stop=True)
                    filled(ins, "m", f"ff{n}", i)
                for b in range(2):
                    after(pe, f"c_read0{b}", i)
                    for f in range(FCH):
                        if b == 0 and f % 2 == 0:
                            after(pe, "fh", i, f // 2 + 1, 2)
                        ins = pe.matmul(C_BANK[b][:, 0:D], fh[:, f, b * SEQ:(b + 1) * SEQ], w2[:, f],
                                        start=(f == 0), stop=(f == FCH - 1))
                    ins.then_inc(sem("ffy"), 1)
                turn_tokens("xn2T", xn[2], "xn2", i, i, 2)
                project_q(1, i)
                attention(1, i)
                if not last:
                    front(i + 1, i)
                turn_tokens("xn3T", xn[3], "xn3", i, i, 2)
                freed(pe, "m", "xn3T", i)
                dst = fill(pe, "m", "logit", i)
                for b in range(2):
                    ins = pe.matmul(dst[:, b * EXPERTS:(b + 1) * EXPERTS], xnT[3][:, b * SEQ:(b + 1) * SEQ], gateT[:],
                                    start=True, stop=True)
                filled(ins, "m", "logit", i)

                def gate_up(c):
                    ring, name = ("s", f"gu{c}") if c < ECH else ("m", "shared")
                    rows = 128 if c < ECH else HID
                    dst = fill(pe, ring, name, i)
                    for k, w in enumerate((wg, wu)):
                        ins = pe.matmul(dst[0:rows, k * TOK:(k + 1) * TOK], w[:, c * 128:c * 128 + rows], xnT[3][:],
                                        start=True, stop=True)
                    filled(ins, ring, name, i)

                def spread(c):
                    dst = fill(pe, "t", f"cb{c}", i)
                    filled(pe.matmul(dst[:, 0:TOK], expsel[:, c], combT[:], start=True, stop=True), "t", f"cb{c}", i)

                def down(c):
                    rows = 128 if c < ECH else HID
                    freed(pe, *(("t", f"cb{c}") if c < ECH else ("m", "shared")), i)
                    for b in range(2):
                        if c == 0:
                            after(pe, f"c_read1{b}", i)
                        ins = pe.matmul(C_BANK[b][:, 0:D], hT[0:rows, c % 2, b * SEQ:(b + 1) * SEQ],
                                        wd[:, c] if c < ECH else swd[:], start=(c == 0), stop=(c == ECH))
                    ins.then_inc(sem("down"), 1)

                gate_up(0)
                gate_up(1)
                after(pe, "csp", i, of=3)
                dst = fill(pe, "m", "combT", i)
                for b in range(2):
                    ins = pe.transpose(dst[:].bitcast(BF16)[:, b * SEQ:(b + 1) * SEQ], cspw[:, b], identb[:])
                filled(ins, "m", "combT", i)
                freed(pe, "m", "combT", i)
                spread(0)
                spread(1)
                for c in range(ECH + 1):
                    if 2 <= c + 2 <= ECH:
                        gate_up(c + 2)
                        if c + 2 < ECH:
                            spread(c + 2)
                    down(c)

            body(0, False)
            with pe.Fori(1, PAIRS - 1) as i:
                body(i, False)
            body(PAIRS - 1, True)


def bucket_onehot():
    behind = np.maximum(np.arange(REL) - (SEQ - 1), 0)
    exact = BUCKETS // 2
    f = np.maximum(behind, 1).astype(np.float32)
    large = exact + (np.log(f / np.float32(exact)) / np.float32(np.log(MAX_DISTANCE / exact))
                     * np.float32(BUCKETS - exact)).astype(np.int32)
    bucket = np.where(behind < exact, behind, np.minimum(large, BUCKETS - 1))
    out = np.zeros((BUCKETS, REL + 1), np.float32)
    out[bucket, np.arange(REL)] = 1.0
    return out


def expert_selector():
    out = np.zeros((3, EXPERTS, ECH, 128), np.float32)
    for e in range(EXPERTS):
        first = e * HID
        out[:, e, first // 128, first % 128:first % 128 + HID] = 1.0
    return out.reshape(3 * EXPERTS, ECH, 128)


def kernel(**inputs):
    import numpy as _np
    import concourse.bacc as _bacc
    from concourse import mybir as _mybir
    from concourse.bass_utils import run_bass_kernel_spmd as _run

    a = {k: _np.asarray(v) for k, v in inputs.items()}
    heads_in = lambda w: w.transpose(1, 0, 2).reshape(D, D)
    wq1, wk1, wv1 = (heads_in(a[f"L1_xattn_W{c}"]) for c in "qkv")
    by_dim = lambda w: w.reshape(-1, 2, HALF, DK).swapaxes(2, 3).reshape(w.shape)
    experts_in = lambda w: w.transpose(1, 0, 2).reshape(D, EXPERTS * HID)
    arrays = {
        "x": a["x"],
        "ctx": a["ctx_1024"][:, ::-1],
        "mask": a["mask_1x1xSxS2_bk1"].reshape(SEQ, SEQ)[:, ::-1].view(_np.uint8),
        "wqk": _np.stack([_np.stack([by_dim(a["L0_xattn_Wq"]), by_dim(a["L0_xattn_Wk"])], 1),
                          _np.stack([by_dim(wq1), by_dim(wk1)], 1)], 1),
        "wv": _np.stack([a["L0_xattn_Wv"], wv1], 1),
        "wo": _np.stack([a["L0_xattn_Wo"], a["L1_xattn_Wo"]], 1),
        "bqk": _np.stack([by_dim(a[f"L{l}_xattn_b{c}"].reshape(D)) for l in range(2) for c in "qk"], 1),
        "bv": _np.tile(_np.concatenate([a["L0_xattn_bv"], a["L1_xattn_bv"].reshape(D)]), (2, 1)),
        "rows": _np.stack([_np.tile(a[n], (2, 1)) for n in ("L0_xattn_bo", "L0_ffn_b2", "L1_xattn_bo")]),
        "table": a["L0_xattn_rpe_table"],
        "u1t": a["L0_ffn_U1"].T,
        "v1": a["L0_ffn_V1"],
        "b1": a["L0_ffn_b1"].reshape(FCH, 128).T,
        "u2t": a["L0_ffn_U2"].T,
        "v2": a["L0_ffn_V2"],
        "gate": a["L1_ffn_gate_w"],
        "wg": _np.concatenate([experts_in(a["L1_ffn_w_gate"]), a["L1_ffn_sw_gate"]], 1),
        "wu": _np.concatenate([experts_in(a["L1_ffn_w_up"]), a["L1_ffn_sw_up"]], 1),
        "wd": a["L1_ffn_w_down"].reshape(ECH, 128, D).transpose(1, 0, 2),
        "swd": a["L1_ffn_sw_down"],
        "ident": _np.eye(128, dtype=_np.float32),
        "onehot": bucket_onehot(),
        "expsel": expert_selector(),
    }
    arrays = {f"in_{k}": _np.ascontiguousarray(v) for k, v in arrays.items()}
    nc = _bacc.Bacc("TRN2", target_bir_lowering=False, num_devices=1)
    args = [nc.dram_tensor(k, v.shape, _mybir.dt.from_np(v.dtype), kind="ExternalInput").ap() for k, v in arrays.items()]
    args.append(nc.dram_tensor("out_0", (BATCH, SEQ, D), _mybir.dt.float32, kind="ExternalOutput").ap())
    bass_xattn_ffn_moe(nc, *args)
    r = _run(nc, [arrays], core_ids=[0])
    return r.results[0]["out_0"]
```

```python
from contextlib import ExitStack

import numpy as np

import concourse.bass as bass
from concourse import mybir

F32 = mybir.dt.float32
BF16 = mybir.dt.bfloat16
U8 = mybir.dt.uint8
ACT = mybir.ActivationFunctionType
ALU = mybir.AluOpType
AX = mybir.AxisListType

BATCH, SEQ, D = 8, 128, 128
HEADS, DK = 16, 8
HALF = HEADS // 2
PAIRS = BATCH // 2
TOK = 2 * SEQ
FF, RANK = 512, 32
FCH = FF // 128
EXPERTS, HID, TOPK = 16, 64, 8
ECH = EXPERTS * HID // 128
BUCKETS, MAX_DISTANCE = 32, 512
REL = 2 * SEQ - 1
NEG = -float(2 ** 100)
LN_EPS, L2_EPS = 1e-5, 1e-12
GELU_C, GELU_A = 0.7978845608028654, 0.044715
SCALE = float(DK) ** -0.5

Q_PART = (0, 0, 0, 1, 1, 2)
K_PART = (0, 1, 2, 0, 1, 0)
PRODS = len(Q_PART)
HROWS = PRODS * DK
SROWS = 2 * HROWS
QROWS = SROWS + 3
VW = 32


def bass_xattn_ffn_moe(nc, x_d, ctx_d, mask_d, wqk_d, wv_d, wo_d, bqk_d, bv_d, rows_d, table_d, u1t_d, v1_d, b1_d,
                       u2t_d, v2_d, gate_d, wg_d, wu_d, wd_d, swd_d, ident_d, onehot_d, expsel_d, out_d):
    rel_d = nc.dram_tensor("rel_bias_scratch", (HEADS, REL + 1), F32, kind="Internal").ap()

    with ExitStack() as ctx:
        def sb(name, shape, dt=F32):
            return ctx.enter_context(nc.sbuf_tensor(name, shape, dt))

        sems = {}

        def sem(name):
            if name not in sems:
                sems[name] = ctx.enter_context(nc.semaphore(name))
            return sems[name]

        def after(eng, name, p, n=None, of=1):
            n = of if n is None else n
            v = p * of + n
            if not (isinstance(v, int) and v <= 0):
                eng.wait_ge(sem(name), v)

        def before(eng, name, p, of=1):
            if not (isinstance(p, int) and p == 0):
                eng.wait_ge(sem(name), p * of)

        bank = [ctx.enter_context(nc.psum_tensor(f"bank{i}", [128, 512], F32)) for i in range(8)]
        Y_BANK = bank[7]

        FRONT = ["xcT", "k", "q0", "v"]
        MOE = ["xn3T", "logit", "combT", "shared"] + [f"{n}{c}" for n in ("gu", "cb") for c in range(ECH)]
        BODY = {
            "m": ["xn3T", "logit", "nmT00", "nmT01", "C00", "C01", "combT", "o0", "xn1T", "xcT", "ff0", "ff1", "k",
                  "q0", "v", "ffy", "xn2T", "q1", "shared", "nmT10", "nmT11", "C10", "C11", "o1"],
            "s": [f"S0{b}{c}" for b in range(2) for c in range(4)] + [f"gu{c}" for c in range(ECH)]
                 + [f"S1{b}{c}" for b in range(2) for c in range(4)],
            "t": [f"T0{b}{c}" for b in range(2) for c in range(4)] + [f"cb{c}" for c in range(ECH)]
                 + [f"T1{b}{c}" for b in range(2) for c in range(4)],
        }
        BANKS = {"m": bank[4:7], "s": bank[0:2], "t": bank[2:4]}
        SETUP = {"m": ["w1", "w2", "rel0", "maskT", "gateT"] + FRONT, "s": [], "t": []}

        def uses(ring, turn):
            if isinstance(turn, str) and turn == "setup":
                return SETUP[ring]
            if isinstance(turn, str):
                return [u for u in BODY[ring] if u in MOE]
            skip = MOE if isinstance(turn, int) and turn == 0 else FRONT if isinstance(turn, int) and turn == PAIRS - 1 else []
            return [u for u in BODY[ring] if u not in skip]

        def number(ring, name, turn):
            k, body = len(BANKS[ring]), BODY[ring]
            assert len(body) % k == 0
            n = uses(ring, turn).index(name)
            if isinstance(turn, str) and turn == "setup":
                return n % k, n // k
            if isinstance(turn, int) and turn == 0:
                n += len(SETUP[ring])
                return n % k, n // k
            n += len(SETUP[ring]) + len(uses(ring, 0))
            if isinstance(turn, str):
                n += len(body) * (PAIRS - 2) + len(uses(ring, PAIRS - 1))
                return n % k, n // k
            return n % k, turn * (len(body) // k) + (n // k - len(body) // k)

        def fill(pe, ring, name, turn):
            k, n = number(ring, name, turn)
            if not (isinstance(n, int) and n == 0):
                pe.wait_ge(sem(f"{ring}_free{k}"), n)
            return BANKS[ring][k]

        def filled(ins, ring, name, turn):
            ins.then_inc(sem(f"{ring}_full{number(ring, name, turn)[0]}"), 1)

        def read(eng, ring, name, turn):
            k, n = number(ring, name, turn)
            eng.wait_ge(sem(f"{ring}_full{k}"), n + 1)
            return BANKS[ring][k]

        def free(ins, ring, name, turn):
            ins.then_inc(sem(f"{ring}_free{number(ring, name, turn)[0]}"), 1)

        def freed(eng, ring, name, turn):
            k, n = number(ring, name, turn)
            eng.wait_ge(sem(f"{ring}_free{k}"), n + 1)

        wqk = sb("wqk", [128, 2, 2, D])
        wv = sb("wv", [128, 2, D])
        wo = sb("wo", [128, 2, D])
        bqk = sb("bqk", [128, 4])
        bqs = sb("bqs", [128, 2])
        bvb = sb("bvb", [128, 2, 2 * D])
        rowb = sb("rowb", [128, 3, 2, D])
        table = sb("table", [BUCKETS, HEADS])
        onehot = sb("onehot", [BUCKETS, REL + 1])
        u1t = sb("u1t", [RANK, D])
        v1 = sb("v1", [RANK, FF])
        b1 = sb("b1", [128, FCH])
        u2t = sb("u2t", [RANK, FF])
        v2 = sb("v2", [RANK, D])
        w1 = sb("w1", [128, FF])
        w2 = sb("w2", [128, FCH, D])
        gate = sb("gate", [EXPERTS, D])
        gsq = sb("gsq", [EXPERTS, D])
        gss = sb("gss", [EXPERTS, 2])
        gateT = sb("gateT", [128, EXPERTS])
        wg = sb("wg", [128, EXPERTS * HID + HID])
        wu = sb("wu", [128, EXPERTS * HID + HID])
        wd = sb("wd", [128, ECH, D])
        swd = sb("swd", [HID, D])
        ident = sb("ident", [128, 128])
        identb = sb("identb", [128, 128], BF16)
        expself = sb("expself", [3 * EXPERTS, ECH, 128])
        expsel = sb("expsel", [3 * EXPERTS, ECH, 128], BF16)
        mask8 = sb("mask8", [SEQ, SEQ], U8)
        maskn = sb("maskn", [SEQ, SEQ])
        masknT = sb("masknT", [SEQ, SEQ])
        relrow = sb("relrow", [HEADS, REL + 1])
        biasq = sb("biasq", [SEQ, HALF, 2, SEQ])
        biask = sb("biask", [SEQ, HALF, 2, SEQ])
        half = sb("half", [128, 4])

        x0 = sb("x0", [128, 2, D])
        cx = sb("cx", [128, 2, D])
        res = [sb(f"res{n}", [128, 2, D]) for n in range(4)]
        xs = [None] + [sb(f"x{n}", [128, 2, D]) for n in range(1, 4)]
        xout = sb("xout", [128, 2, D])
        xn = [sb(f"xn{n}", [128, 2, D]) for n in range(4)]
        xnT = [sb(f"xnT{n}", [128, TOK]) for n in range(4)]
        xcT = sb("xcT_sb", [128, 2, TOK])
        stats = sb("stats", [128, 4, 2, 6])
        mv = sb("mv", [128, 4, 2, 2])
        ve = sb("ve", [128, 4, 2])
        rstd = sb("rstd", [128, 4, 2])
        dummy = sb("tiny", [128, 4])
        qf = sb("qf", [128, 2, TOK])
        qr = sb("qr", [128, 2, TOK])
        qsp = sb("qsp", [128, 3, 2, TOK], BF16)
        kf = sb("kf", [128, 2, TOK])
        kr = sb("kr", [128, 2, TOK])
        ksp = sb("ksp", [128, 3, 2, TOK], BF16)
        qz = [sb(f"qz{l}", [QROWS, HALF, 2, TOK], BF16) for l in range(2)]
        kst = [sb(f"kst{l}", [QROWS, HALF, TOK], BF16) for l in range(2)]
        vf = sb("vf", [128, 2 * TOK])
        va = sb("va", [128, 2, 2, HEADS, VW])
        es = sb("es", [128, 2, 512])
        et = sb("et", [128, 4, 512])
        mx = sb("mx", [128, 2, HEADS])
        mr = sb("mr", [128, 2, HEADS])
        nmw = sb("nm", [128, 2, 128], BF16)
        nm = nmw[:, :, 0:3 * HEADS].rearrange("p b (n h) -> p b n h", n=3)
        nmT = sb("nmT_sb", [3 * HEADS, 2, SEQ], BF16)
        pt = sb("pt", [128, 2, HEADS, SEQ])
        ct1 = sb("ct1", [128, 2, 4, 4, 32])
        crc = sb("crc", [128, 2, 4, 4])
        ct2 = sb("ct2", [128, 2, 4, 4, DK])
        ct3 = sb("ct3", [128, 2, SEQ])
        fv = sb("fv", [128, FCH, TOK])
        fs = sb("fs", [128, FCH, TOK])
        fw = sb("fw", [128, FCH, TOK])
        fh = sb("fh", [128, FCH, TOK])
        sq = sb("sq", [128, 2, D])
        ss = sb("ss", [128, 2])
        sc = sb("sc", [128, 2])
        rn = sb("rn", [128, 2])
        lg = sb("lg", [128, 2, EXPERTS])
        top = sb("top", [128, 2, TOPK])
        lr = sb("lr", [128, 2, EXPERTS])
        sel = sb("sel", [128, 2, EXPERTS])
        th = sb("th", [128, 2, EXPERTS])
        sw = sb("sw", [128, 2, EXPERTS])
        sws = sb("sws", [128, 2])
        swr = sb("swr", [128, 2])
        comb = sb("comb", [128, 2, EXPERTS])
        cr = sb("cr", [128, 2, EXPERTS])
        cspw = sb("csp", [128, 2, 128], BF16)
        csp = cspw[:, :, 0:3 * EXPERTS].rearrange("p b (n e) -> p b n e", n=3)
        combT = sb("combT_sb", [3 * EXPERTS, TOK], BF16)
        gth = sb("gth", [128, 2, TOK])
        ga = sb("ga", [128, 2, TOK])
        gb = sb("gb", [128, 2, TOK])
        hT = sb("hT", [128, 2, TOK])

        block = ctx.enter_context(nc.Block())

        @block.sync
        def _(sp):
            def load_pair(p):
                sp.dma_start(x0[:], x_d[bass.ds(2 * p, 2)].rearrange("b s d -> s b d")).then_inc(sem("x0_in"), 16)
                sp.dma_start(cx[:], ctx_d[bass.ds(2 * p, 2)].rearrange("b s d -> s b d")).then_inc(sem("cx_in"), 16)

            def stack_q(l, p):
                after(sp, f"q_split{l}", p)
                for hh in range(2):
                    for n, part in enumerate(Q_PART):
                        r = HROWS * hh + DK * n
                        sp.dma_start(qz[l][r:r + DK, :, hh, :],
                                     qsp[64 * hh:64 * hh + 64, part, l, :]).then_inc(sem(f"qz{l}_in"), 16)

            def stack_k(l, p, turn, stored=None):
                if l == 0:
                    after(sp, "k_split", p)
                elif not isinstance(turn, str):
                    read(sp, "t", "T113", turn)
                for hh in range(2):
                    for n, part in enumerate(K_PART):
                        if n == 1 and hh == 0 and stored is not None:
                            after(sp, "stored", stored, of=16)
                        r = HROWS * hh + DK * n
                        sp.dma_start(kst[l][r:r + DK, :, :],
                                     ksp[64 * hh:64 * hh + 64, part, l, :]).then_inc(sem(f"kst{l}_in"), 16)

            def max_rows(l, i):
                for b in range(2):
                    freed(sp, "m", f"nmT{l}{b}", i)
                    sp.dma_start(qz[l][SROWS:QROWS, :, :, b * SEQ:(b + 1) * SEQ],
                                 nmT[:, b, :]).then_inc(sem(f"max_in{b}"), 16)

            sp.dma_start(ident[:], ident_d).then_inc(sem("ident_in"), 16)
            load_pair(0)
            sp.dma_start(wqk[:], wqk_d).then_inc(sem("proj_in"), 16)
            sp.dma_start(wv[:], wv_d).then_inc(sem("proj_in"), 16)
            sp.dma_start(bqk[:], bqk_d).then_inc(sem("bqk_in"), 16)
            sp.dma_start(table[:], table_d).then_inc(sem("rel_in"), 16)
            sp.dma_start(onehot[:], onehot_d).then_inc(sem("rel_in"), 16)
            sp.dma_start(mask8[:], mask_d).then_inc(sem("mask_in"), 16)
            sp.dma_start(u1t[:], u1t_d).then_inc(sem("ffw_in"), 16)
            sp.dma_start(v1[:], v1_d).then_inc(sem("ffw_in"), 16)
            sp.dma_start(u2t[:], u2t_d).then_inc(sem("ffw_in"), 16)
            sp.dma_start(v2[:], v2_d).then_inc(sem("ffw_in"), 16)
            sp.dma_start(gate[:], gate_d).then_inc(sem("gate_in"), 16)
            sp.dma_start(bvb[:], bv_d.partition_broadcast(128)).then_inc(sem("bias_in"), 16)
            sp.dma_start(rowb[:], rows_d.partition_broadcast(128)).then_inc(sem("bias_in"), 16)
            freed(sp, "m", "rel0", "setup")
            sp.dma_start(rel_d, relrow[:]).then_inc(sem("rel_out"), 16)
            sp.wait_ge(sem("rel_out"), 16)
            for tile in (biasq, biask):
                for hh in range(2):
                    src = bass.AP(tensor=rel_d.tensor, offset=HALF * hh * (REL + 1),
                                  ap=[[1, SEQ], [REL + 1, HALF], [1, SEQ]])
                    sp.dma_start(tile[:, :, hh, :], src).then_inc(sem("biasqk_in"), 16)
            sp.wait_ge(sem("stacks_cleared"), 2)
            sp.wait_ge(sem("kst_ones"), 2)
            stack_k(0, 0, "setup")
            stack_q(0, 0)
            sp.dma_start(b1[:], b1_d).then_inc(sem("b1_in"), 16)
            sp.dma_start(expself[:], expsel_d).then_inc(sem("expsel_in"), 16)
            sp.dma_start(wo[:], wo_d).then_inc(sem("wo_in"), 16)
            stack_k(1, 0, "setup")
            sp.dma_start(wg[:], wg_d).then_inc(sem("moe_in"), 16)
            sp.dma_start(wu[:], wu_d).then_inc(sem("moe_in"), 16)
            sp.dma_start(wd[:], wd_d).then_inc(sem("moe_in"), 16)
            sp.dma_start(swd[:], swd_d).then_inc(sem("moe_in"), 16)

            def store(p, first):
                after(sp, "xout", p, of=2)
                sp.dma_start(out_d[bass.ds(first, 2)].rearrange("b s d -> s b d"), xout[:]).then_inc(sem("stored"), 16)

            def body(i):
                first = 2 * (i - 1) if isinstance(i, int) else sp.snap(2 * i - 2)
                last = isinstance(i, int) and i == PAIRS - 1
                if not last:
                    load_pair(i + 1)
                max_rows(0, i)
                if not last:
                    stack_k(0, i + 1, i)
                stack_q(1, i)
                max_rows(1, i)
                if not (isinstance(i, int) and i == 0):
                    store(i - 1, first)
                if not last:
                    stack_q(0, i + 1)
                    stack_k(1, i + 1, i, None if isinstance(i, int) and i == 0 else i - 1)
                else:
                    after(sp, "stored", i - 1, of=16)

            after(sp, "res0", 0)
            body(0)
            with sp.Fori(1, PAIRS - 1) as i:
                body(i)
            body(PAIRS - 1)
            store(PAIRS - 1, 2 * (PAIRS - 1))
            after(sp, "stored", PAIRS - 1, of=16)

        @block.gpsimd
        def _(pool):
            def power(n, p):
                after(pool, f"ve{n}", p)
                pool.tensor_tensor(rstd[:, n, :], ve[:, n, :], half[:, 0:2], ALU.pow).then_inc(sem(f"rstd{n}"), 1)

            def residual(n, src):
                pool.tensor_tensor(res[n][:], src[:], rowb[:, n], ALU.add).then_inc(sem(f"res{n}"), 1)

            def split_q(l, p, turn):
                freed(pool, "m", f"q{l}", turn)
                pool.tensor_tensor(qr[:, l], qf[:, l], qsp[:, 0, l], ALU.subtract).then_inc(sem(f"q_rest{l}"), 1)
                after(pool, f"q_mid{l}", p)
                pool.tensor_tensor(qsp[:, 2, l], qr[:, l], qsp[:, 1, l], ALU.subtract).then_inc(sem(f"q_split{l}"), 1)

            def split_k(p, turn):
                freed(pool, "m", "k", turn)
                pool.tensor_tensor(kr[:], kf[:], ksp[:, 0], ALU.subtract).then_inc(sem("k_rest"), 1)
                after(pool, "k_mid", p)
                pool.tensor_tensor(ksp[:, 2], kr[:], ksp[:, 1], ALU.subtract).then_inc(sem("k_split"), 1)

            def add_value_bias(p, turn):
                if not isinstance(turn, str):
                    read(pool, "m", "C11", turn)
                freed(pool, "m", "v", turn)
                pool.tensor_tensor(va[:, :, :, :, 0:DK].rearrange("p b l h d -> p (b l h) d"),
                                   vf[:].rearrange("p (n d) -> p n d", d=DK),
                                   bvb[:].rearrange("p b (n d) -> p (b n) d", d=DK), ALU.add).then_inc(sem("va"), 1)

            def router_norm(p):
                after(pool, "ss_clamped", p)
                pool.tensor_tensor(rn[:], sc[:], half[:, 0:2], ALU.pow).then_inc(sem("rn"), 1)

            pool.memset(half[:], -0.5).then_inc(sem("half"), 1)
            pool.wait_ge(sem("half"), 1)
            power(0, 0)
            pool.wait_ge(sem("gss"), 1)
            pool.tensor_tensor(gss[:, 1:2], gss[:, 0:1], half[0:EXPERTS, 0:1], ALU.pow).then_inc(sem("gate_norm"), 1)
            split_k(0, "setup")
            split_q(0, 0, "setup")
            pool.wait_ge(sem("bias_in"), 32)
            after(pool, "x0_in", 0, of=16)
            residual(0, x0)
            pool.wait_ge(sem("va_cleared"), 1)
            add_value_bias(0, "setup")

            def body(i):
                first = isinstance(i, int) and i == 0
                last = isinstance(i, int) and i == PAIRS - 1
                if not first:
                    router_norm(i - 1)
                freed(pool, "m", "o0", i)
                residual(1, xs[1])
                power(1, i)
                if not last:
                    power(0, i + 1)
                    after(pool, "x0_in", i + 1, of=16)
                    residual(0, x0)
                    split_k(i + 1, i)
                    split_q(0, i + 1, i)
                power(2, i)
                residual(2, xs[2])
                split_q(1, i, i)
                if not last:
                    add_value_bias(i + 1, i)
                power(3, i)

            body(0)
            with pool.Fori(1, PAIRS - 1) as i:
                body(i)
            body(PAIRS - 1)
            router_norm(PAIRS - 1)

        @block.scalar
        def _(act):
            def copy_turned(dst, name, turn):
                src = read(act, "m", name, turn)
                free(act.activation(dst, src[:, 0:TOK], ACT.Copy), "m", name, turn)

            def copy_front(turn):
                src = read(act, "m", "xcT", turn)
                free(act.activation(xcT[:], src[:], ACT.Copy), "m", "xcT", turn)

            def project_q(l, p, turn):
                src = read(act, "m", f"q{l}", turn)[:, 0:TOK]
                before(act, f"qz{l}_in", p, of=2 * PRODS * 16)
                act.activation(qf[:, l], src, ACT.Identity, bias=bqs[:, l:l + 1], scale=SCALE)
                free(act.activation(qsp[:, 0, l], src, ACT.Identity, bias=bqs[:, l:l + 1], scale=SCALE),
                     "m", f"q{l}", turn)

            def middle_q(l, p):
                after(act, f"q_rest{l}", p)
                act.activation(qsp[:, 1, l], qr[:, l], ACT.Copy).then_inc(sem(f"q_mid{l}"), 1)

            def project_k(p, turn):
                src = read(act, "m", "k", turn)
                before(act, "kst1_in", p, of=2 * PRODS * 16)
                for l in range(2):
                    for dst in (kf[:, l], ksp[:, 0, l]):
                        ins = act.activation(dst, src[:, l * TOK:(l + 1) * TOK], ACT.Identity,
                                             bias=bqk[:, 2 * l + 1:2 * l + 2])
                free(ins, "m", "k", turn)

            def middle_k(p):
                after(act, "k_rest", p)
                act.activation(ksp[:, 1], kr[:], ACT.Copy).then_inc(sem("k_mid"), 1)

            def copy_v(p, turn):
                src = read(act, "m", "v", turn)
                before(act, "va", p)
                free(act.activation(vf[:], src[:], ACT.Copy), "m", "v", turn)

            def max_turned(l, b, i):
                src = read(act, "m", f"nmT{l}{b}", i)
                v = src[:].bitcast(BF16)[0:3 * HEADS, 0:SEQ]
                if l:
                    after(act, f"max_in{b}", i, 16, 32)
                else:
                    before(act, f"max_in{b}", i, of=32)
                free(act.activation(nmT[:, b], v, ACT.Copy), "m", f"nmT{l}{b}", i)

            def softmax(l, b, i):
                for c in range(4):
                    dst = pt[:, b, 4 * c:4 * c + 4, :]
                    if l == 0:
                        freed(act, "t", f"T0{b}{c}", i)
                        act.activation(dst, et[:, c, :], ACT.Exp).then_inc(sem(f"p0{b}"), 1)
                    else:
                        src = read(act, "t", f"T1{b}{c}", i)
                        free(act.activation(dst, src[:], ACT.Exp), "t", f"T1{b}{c}", i)

            def gelu_input(n, i):
                src = read(act, "m", f"ff{n}", i)
                for k in range(2):
                    f = 2 * n + k
                    ins = act.activation(fv[:, f], src[:, k * TOK:(k + 1) * TOK], ACT.Identity, bias=b1[:, f:f + 1])
                free(ins, "m", f"ff{n}", i)
                freed(act, "m", f"ff{n}", i)
                act.activation(fs[:, 2 * n:2 * n + 2], fv[:, 2 * n:2 * n + 2], ACT.Square).then_inc(sem("fsq"), 1)

            def gelu_tanh(n, i):
                after(act, "fw", i, n + 1, 2)
                act.activation(fs[:, 2 * n:2 * n + 2], fw[:, 2 * n:2 * n + 2], ACT.Tanh, scale=GELU_C)\
                   .then_inc(sem("ftanh"), 1)

            def router_squares(p):
                after(act, "xn3", p, of=2)
                for b in range(2):
                    act.activation(sq[:, b], xn[3][:, b], ACT.Square, accum_out=ss[:, b:b + 1]).then_inc(sem("ss"), 1)

            def router_tanh(p, turn):
                freed(act, "m", "logit", turn)
                act.activation(th[:], lg[:], ACT.Tanh, scale=0.5).then_inc(sem("th"), 1)

            def copy_comb(turn):
                src = read(act, "m", "combT", turn)
                v = src[:].bitcast(BF16)[0:3 * EXPERTS, 0:TOK]
                free(act.activation(combT[:], v, ACT.Copy), "m", "combT", turn)

            def gate_tanh(c, p, turn):
                if c >= 2:
                    after(act, "ga", p, c - 1, ECH + 1)
                if c < ECH:
                    src, rows = read(act, "s", f"gu{c}", turn), 128
                else:
                    src, rows = read(act, "m", "shared", turn), HID
                act.activation(gth[0:rows, c % 2], src[0:rows, 0:TOK], ACT.Tanh, scale=0.5).then_inc(sem("gth"), 1)

            act.wait_ge(sem("bqk_in"), 16)
            act.activation(bqs[:], bqk[:].rearrange("p (l n) -> p n l", n=2)[:, 0, :], ACT.Copy, scale=SCALE)\
               .then_inc(sem("bqs"), 1)
            act.wait_ge(sem("gate_in"), 16)
            act.activation(gsq[:], gate[:], ACT.Square, accum_out=gss[:, 0:1]).then_inc(sem("gsq"), 1)
            act.wait_ge(sem("bqs"), 1)
            copy_front("setup")
            project_k(0, "setup")
            project_q(0, 0, "setup")
            middle_k(0)
            middle_q(0, 0)
            copy_v(0, "setup")
            act.wait_ge(sem("b1_in"), 16)

            def body(i):
                p = i - 1
                first = isinstance(i, int) and i == 0
                last = isinstance(i, int) and i == PAIRS - 1
                if not first:
                    router_squares(p)
                    copy_turned(xnT[3][:], "xn3T", i)
                max_turned(0, 0, i)
                max_turned(0, 1, i)
                softmax(0, 0, i)
                if not first:
                    gate_tanh(0, p, i)
                    gate_tanh(1, p, i)
                    router_tanh(p, i)
                softmax(0, 1, i)
                if not first:
                    copy_comb(i)
                    gate_tanh(2, p, i)
                copy_turned(xnT[1][:], "xn1T", i)
                if not last:
                    copy_front(i)
                gelu_input(0, i)
                gelu_input(1, i)
                if not first:
                    gate_tanh(3, p, i)
                gelu_tanh(0, i)
                if not last:
                    project_k(i + 1, i)
                gelu_tanh(1, i)
                if not last:
                    project_q(0, i + 1, i)
                    middle_k(i + 1)
                    middle_q(0, i + 1)
                    copy_v(i + 1, i)
                if not first:
                    gate_tanh(4, p, i)
                    gate_tanh(5, p, i)
                copy_turned(xnT[2][:], "xn2T", i)
                project_q(1, i, i)
                middle_q(1, i)
                if not first:
                    for c in range(6, ECH + 1):
                        gate_tanh(c, p, i)
                max_turned(1, 0, i)
                max_turned(1, 1, i)
                softmax(1, 0, i)
                softmax(1, 1, i)

            body(0)
            with act.Fori(1, PAIRS - 1) as i:
                body(i)
            body(PAIRS - 1)
            p = PAIRS - 1
            router_squares(p)
            copy_turned(xnT[3][:], "xn3T", "tail")
            gate_tanh(0, p, "tail")
            gate_tanh(1, p, "tail")
            router_tanh(p, "tail")
            copy_comb("tail")
            for c in range(2, ECH + 1):
                gate_tanh(c, p, "tail")

        @block.vector
        def _(dve):
            def variance(n, src, p):
                for b in range(2):
                    dve.bn_stats(stats[:, n, b], src[:, b]).then_inc(sem(f"stats{n}"), 1)
                after(dve, f"stats{n}", p, of=2)
                dve.tensor_copy(dummy[:, 1:2], half[:, 0:1]).then_inc(sem("wait_carried"), 1)
                for b in range(2):
                    dve.bn_aggr(mv[:, n, b], stats[:, n, b]).then_inc(sem(f"mv{n}"), 1)
                after(dve, f"mv{n}", p, of=2)
                dve.tensor_scalar(ve[:, n], mv[:, n, :, 1], LN_EPS, None, ALU.add).then_inc(sem(f"ve{n}"), 1)

            def normalize(n, src, p):
                after(dve, f"rstd{n}", p)
                for b in range(2):
                    dve.tensor_scalar(xn[n][:, b], src[:, b], mv[:, n, b, 0:1], rstd[:, n, b:b + 1],
                                      ALU.subtract, ALU.mult).then_inc(sem(f"xn{n}"), 1)

            def row_max(l, b, i):
                for c in range(4):
                    src = read(dve, "s", f"S{l}{b}{c}", i)
                    if l == 0:
                        free(dve.tensor_tensor(es[:, c % 2], src[:], biasq[:, 2 * c:2 * c + 2], ALU.add),
                             "s", f"S{l}{b}{c}", i)
                        freed(dve, "s", f"S{l}{b}{c}", i)
                        src = es[:, c % 2]
                        ins = dve.tensor_reduce(mx[:, b, 4 * c:4 * c + 4], src.rearrange("p (h k) -> p h k", h=4),
                                                AX.X, ALU.max)
                        ins.then_inc(sem(f"mx0{b}"), 1)
                        after(dve, f"mx0{b}", i, c + 1, 4)
                    else:
                        ins = dve.tensor_reduce(mx[:, b, 4 * c:4 * c + 4], src[:].rearrange("p (h k) -> p h k", h=4),
                                                AX.X, ALU.max)
                        free(ins, "s", f"S{l}{b}{c}", i)
                        freed(dve, "s", f"S{l}{b}{c}", i)
                dve.tensor_scalar(nm[:, b, 0], mx[:, b], -1.0, None, ALU.mult).then_inc(sem("nm_a"), 1)
                after(dve, "nm_a", i, 2 * l + b + 1, 4)
                dve.scalar_tensor_tensor(mr[:, b], mx[:, b], -1.0, nm[:, b, 0], ALU.mult, ALU.subtract)\
                   .then_inc(sem("nm_b"), 1)
                after(dve, "nm_b", i, 2 * l + b + 1, 4)
                dve.tensor_copy(nm[:, b, 1], mr[:, b]).then_inc(sem("nm_c"), 1)
                after(dve, "nm_c", i, 2 * l + b + 1, 4)
                dve.tensor_tensor(nm[:, b, 2], mr[:, b], nm[:, b, 1], ALU.subtract).then_inc(sem(f"nm{l}{b}"), 1)

            def add_bias(b, i):
                for c in range(4):
                    src = read(dve, "t", f"T0{b}{c}", i)
                    if b:
                        after(dve, "p00", i, c + 1, 4)
                    else:
                        before(dve, "p01", i, of=4)
                    free(dve.tensor_tensor(et[:, c], src[:], biask[:, 2 * c:2 * c + 2], ALU.add),
                         "t", f"T0{b}{c}", i)

            def context(l, b, i):
                src = read(dve, "m", f"C{l}{b}", i)
                free(dve.transpose(ct1[:, b], src[:]), "m", f"C{l}{b}", i)
                freed(dve, "m", f"C{l}{b}", i)
                dve.reciprocal(crc[:, b], ct1[:, b, :, :, DK]).then_inc(sem("crc"), 1)
                after(dve, "crc", i, 2 * l + b + 1, 4)
                dve.tensor_tensor(ct2[:, b].rearrange("p q g d -> p g q d"), ct1[:, b, :, :, 0:DK],
                                  crc[:, b].unsqueeze(3).broadcast_to([128, 4, 4, DK]), ALU.mult)\
                   .then_inc(sem("ct2"), 1)
                after(dve, "ct2", i, 2 * l + b + 1, 4)
                dve.transpose(ct3[:, b], ct2[:, b]).then_inc(sem(f"ct3{l}"), 1)

            def add_residual(l, i):
                n = 1 if l == 0 else 3
                src = read(dve, "m", f"o{l}", i)
                after(dve, f"res{n - 1}", i)
                free(dve.tensor_tensor(xs[n][:], src[:, 0:TOK].rearrange("p (b d) -> p b d", b=2), res[n - 1][:],
                                       ALU.add), "m", f"o{l}", i)
                freed(dve, "m", f"o{l}", i)

            def gelu_argument(n, i):
                after(dve, "fsq", i, n + 1, 2)
                h = slice(2 * n, 2 * n + 2)
                dve.tensor_scalar(fw[:, h], fs[:, h], GELU_A, 1.0, ALU.mult, ALU.add).then_inc(sem("fw_a"), 1)
                after(dve, "fw_a", i, n + 1, 2)
                dve.tensor_tensor(fw[:, h], fw[:, h], fv[:, h], ALU.mult).then_inc(sem("fw"), 1)

            def gelu_output(n, i):
                after(dve, "ftanh", i, n + 1, 2)
                h = slice(2 * n, 2 * n + 2)
                dve.scalar_tensor_tensor(fh[:, h], fs[:, h], 1.0, fv[:, h], ALU.add, ALU.mult).then_inc(sem("fh"), 1)

            def add_ffn(i):
                src = read(dve, "m", "ffy", i)
                after(dve, "res1", i)
                free(dve.tensor_tensor(xs[2][:], src[:, 0:TOK].rearrange("p (b d) -> p b d", b=2), res[1][:],
                                       ALU.add), "m", "ffy", i)
                freed(dve, "m", "ffy", i)

            def router_clamp(p):
                after(dve, "ss", p, of=2)
                dve.tensor_scalar(sc[:], ss[:], L2_EPS * L2_EPS, None, ALU.max).then_inc(sem("ss_clamped"), 1)

            def router_best(p, turn):
                src = read(dve, "m", "logit", turn)
                after(dve, "rn", p)
                for b in range(2):
                    ins = dve.tensor_scalar(lg[:, b], src[:, b * EXPERTS:(b + 1) * EXPERTS], rn[:, b:b + 1], None,
                                            ALU.mult)
                free(ins, "m", "logit", turn)
                freed(dve, "m", "logit", turn)
                dve.tensor_copy(dummy[:, 2:3], half[:, 0:1]).then_inc(sem("wait_carried"), 1)
                for b in range(2):
                    dve.max(top[:, b], lg[:, b]).then_inc(sem("top"), 1)
                after(dve, "top", p, of=2)
                dve.tensor_copy(dummy[:, 3:4], half[:, 0:1]).then_inc(sem("wait_carried"), 1)
                for b in range(2):
                    dve.match_replace(lr[:, b], top[:, b], lg[:, b], -1e30).then_inc(sem("lr"), 1)
                after(dve, "lr", p, of=2)
                dve.tensor_tensor(sel[:], lr[:], lg[:], ALU.not_equal).then_inc(sem("sel"), 1)

            def router_weights(p):
                after(dve, "sel", p)
                after(dve, "th", p)
                dve.scalar_tensor_tensor(sw[:], th[:], 1.0, sel[:], ALU.add, ALU.mult).then_inc(sem("sw"), 1)
                after(dve, "sw", p)
                dve.tensor_reduce(sws[:], sw[:], AX.X, ALU.add).then_inc(sem("sws"), 1)
                after(dve, "sws", p)
                dve.reciprocal(swr[:], sws[:]).then_inc(sem("swr"), 1)
                after(dve, "swr", p)
                for b in range(2):
                    dve.tensor_scalar(comb[:, b], sw[:, b], swr[:, b:b + 1], 0.5, ALU.mult, ALU.mult)\
                       .then_inc(sem("comb"), 1)
                after(dve, "comb", p, of=2)
                dve.tensor_copy(csp[:, :, 0], comb[:]).then_inc(sem("csp"), 1)
                after(dve, "csp", p, 1, 3)
                dve.tensor_tensor(cr[:], comb[:], csp[:, :, 0], ALU.subtract).then_inc(sem("cr"), 1)
                after(dve, "cr", p)
                dve.tensor_copy(csp[:, :, 1], cr[:]).then_inc(sem("csp"), 1)
                after(dve, "csp", p, 2, 3)
                dve.tensor_tensor(csp[:, :, 2], cr[:], csp[:, :, 1], ALU.subtract).then_inc(sem("csp"), 1)

            def hidden(c, p, turn):
                rows, k = (128 if c < ECH else HID), c % 2
                after(dve, "gth", p, c + 1, ECH + 1)
                src = read(dve, "s", f"gu{c}", turn) if c < ECH else read(dve, "m", "shared", turn)
                dve.scalar_tensor_tensor(ga[0:rows, k], gth[0:rows, k], 1.0, src[0:rows, 0:TOK], ALU.add, ALU.mult)\
                   .then_inc(sem("ga"), 1)
                after(dve, "ga", p, c + 1, ECH + 1)
                if c >= 2:
                    after(dve, "down", p, c - 1, ECH + 1)
                if c < ECH:
                    free(dve.tensor_tensor(gb[:, k], ga[:, k], src[:, TOK:2 * TOK], ALU.mult), "s", f"gu{c}", turn)
                    freed(dve, "s", f"gu{c}", turn)
                    src = read(dve, "t", f"cb{c}", turn)
                    free(dve.tensor_tensor(hT[:, k], gb[:, k], src[:, 0:TOK], ALU.mult), "t", f"cb{c}", turn)
                else:
                    free(dve.scalar_tensor_tensor(hT[0:rows, k], ga[0:rows, k], 0.5, src[0:rows, TOK:2 * TOK],
                                                  ALU.mult, ALU.mult), "m", "shared", turn)

            def output(p):
                after(dve, "down", p, of=ECH + 1)
                for b in range(2):
                    dve.tensor_tensor(xout[:, b], Y_BANK[:, b * D:(b + 1) * D], xs[3][:, b], ALU.add)\
                       .then_inc(sem("xout"), 1)

            dve.memset(nmw[:], 0.0).then_inc(sem("pads"), 1)
            dve.memset(cspw[:], 0.0).then_inc(sem("pads"), 1)
            dve.wait_ge(sem("half"), 1)
            after(dve, "x0_in", 0, of=16)
            variance(0, x0, 0)
            normalize(0, x0, 0)
            for l in range(2):
                dve.memset(qz[l][:], 0.0).then_inc(sem("stacks_cleared"), 1)
                dve.memset(kst[l][64:QROWS], 1.0).then_inc(sem("kst_ones"), 1)
            dve.memset(va[:], 0.0).then_inc(sem("va_zeros"), 1)
            dve.wait_ge(sem("va_zeros"), 1)
            dve.memset(va[:, :, :, :, DK:DK + 1], 1.0).then_inc(sem("va_cleared"), 1)
            dve.wait_ge(sem("ident_in"), 16)
            dve.tensor_copy(identb[:], ident[:]).then_inc(sem("identb"), 1)
            dve.wait_ge(sem("gsq"), 1)
            dve.tensor_scalar(gss[:, 0:1], gss[:, 0:1], L2_EPS * L2_EPS, None, ALU.max).then_inc(sem("gss"), 1)
            dve.wait_ge(sem("gate_norm"), 1)
            dve.tensor_scalar(gsq[:], gate[:], gss[:, 1:2], None, ALU.mult).then_inc(sem("gate_normed"), 1)
            dve.wait_ge(sem("mask_in"), 16)
            dve.tensor_scalar(maskn[:], mask8[:], NEG, None, ALU.mult).then_inc(sem("maskn"), 1)
            free(dve.tensor_copy(w1[:], read(dve, "m", "w1", "setup")[:]), "m", "w1", "setup")
            free(dve.tensor_scalar(w2[:], read(dve, "m", "w2", "setup")[:].rearrange("p (n d) -> p n d", n=FCH),
                                   0.5, None, ALU.mult), "m", "w2", "setup")
            src = read(dve, "m", "rel0", "setup")
            free(dve.tensor_copy(relrow[:], src[0:HEADS, 0:REL + 1]), "m", "rel0", "setup")
            free(dve.tensor_copy(masknT[:], read(dve, "m", "maskT", "setup")[:, 0:SEQ]), "m", "maskT", "setup")
            free(dve.tensor_copy(gateT[:], read(dve, "m", "gateT", "setup")[:, 0:EXPERTS]), "m", "gateT", "setup")
            dve.wait_ge(sem("expsel_in"), 16)
            dve.tensor_copy(expsel[:], expself[:]).then_inc(sem("expsel"), 1)
            dve.wait_ge(sem("biasqk_in"), 64)
            freed(dve, "m", "maskT", "setup")
            for tile, m in ((biasq, maskn), (biask, masknT)):
                v = tile[:].rearrange("p a b k -> p (a b) k")
                dve.tensor_tensor(v, v, m[:].unsqueeze(1).broadcast_to([SEQ, HEADS, SEQ]), ALU.add)\
                   .then_inc(sem("masked"), 1)
            dve.wait_ge(sem("masked"), 2)
            dve.wait_ge(sem("pads"), 2)

            def body(i):
                p = i - 1
                first = isinstance(i, int) and i == 0
                last = isinstance(i, int) and i == PAIRS - 1
                if not first:
                    router_clamp(p)
                row_max(0, 0, i)
                row_max(0, 1, i)
                add_bias(0, i)
                if not first:
                    router_best(p, i)
                add_bias(1, i)
                if not first:
                    router_weights(p)
                context(0, 0, i)
                context(0, 1, i)
                if not first:
                    hidden(0, p, i)
                add_residual(0, i)
                variance(1, xs[1], i)
                if not last:
                    after(dve, "x0_in", i + 1, of=16)
                    variance(0, x0, i + 1)
                normalize(1, xs[1], i)
                if not last:
                    normalize(0, x0, i + 1)
                if not first:
                    hidden(1, p, i)
                gelu_argument(0, i)
                gelu_argument(1, i)
                if not first:
                    hidden(2, p, i)
                gelu_output(0, i)
                gelu_output(1, i)
                if not first:
                    hidden(3, p, i)
                add_ffn(i)
                variance(2, xs[2], i)
                if not first:
                    hidden(4, p, i)
                normalize(2, xs[2], i)
                if not first:
                    for c in range(5, ECH + 1):
                        hidden(c, p, i)
                    output(p)
                row_max(1, 0, i)
                row_max(1, 1, i)
                context(1, 0, i)
                context(1, 1, i)
                add_residual(1, i)
                variance(3, xs[3], i)
                normalize(3, xs[3], i)

            body(0)
            with dve.Fori(1, PAIRS - 1) as i:
                body(i)
            body(PAIRS - 1)
            p = PAIRS - 1
            router_clamp(p)
            router_best(p, "tail")
            router_weights(p)
            for c in range(ECH + 1):
                hidden(c, p, "tail")
            before(dve, "stored", p, of=16)
            output(p)

        @block.tensor
        def _(pe):
            def turn_tokens(n, name, i, turn):
                after(pe, f"xn{n}", i, of=2)
                dst = fill(pe, "m", name, turn)
                for b in range(2):
                    ins = pe.transpose(dst[:, b * SEQ:(b + 1) * SEQ], xn[n][:, b], ident[:])
                filled(ins, "m", name, turn)

            def turn_front(p, turn):
                after(pe, "xn0", p, of=2)
                after(pe, "cx_in", p, of=16)
                dst = fill(pe, "m", "xcT", turn)
                for k, src in enumerate((xn[0], cx)):
                    for b in range(2):
                        t = (2 * k + b) * SEQ
                        ins = pe.transpose(dst[:, t:t + SEQ], src[:, b], ident[:])
                filled(ins, "m", "xcT", turn)

            def keys(turn):
                freed(pe, "m", "xcT", turn)
                dst = fill(pe, "m", "k", turn)
                for l in range(2):
                    ins = pe.matmul(dst[:, l * TOK:(l + 1) * TOK], wqk[:, l, 1], xcT[:, 1], start=True, stop=True)
                filled(ins, "m", "k", turn)

            def queries(l, turn):
                freed(pe, "m", "xn2T" if l else "xcT", turn)
                dst = fill(pe, "m", f"q{l}", turn)
                ins = pe.matmul(dst[:, 0:TOK], wqk[:, l, 0], xnT[2][:] if l else xcT[:, 0], start=True, stop=True)
                filled(ins, "m", f"q{l}", turn)

            def value_rows(turn):
                dst = fill(pe, "m", "v", turn)
                for b in range(2):
                    ins = pe.matmul(dst[:, b * TOK:(b + 1) * TOK], xcT[:, 1, b * SEQ:(b + 1) * SEQ], wv[:],
                                    start=True, stop=True)
                filled(ins, "m", "v", turn)

            def scores(l, b, i):
                if b == 0:
                    after(pe, f"kst{l}_in", i, of=2 * PRODS * 16)
                    after(pe, f"qz{l}_in", i, of=2 * PRODS * 16)
                for c in range(4):
                    dst = fill(pe, "s", f"S{l}{b}{c}", i)
                    for s in range(4):
                        hp, hh = (4 * c + s) // 2, (4 * c + s) % 2
                        tok = slice(b * SEQ, (b + 1) * SEQ)
                        ins = pe.matmul(dst[:, s * SEQ:(s + 1) * SEQ], qz[l][0:SROWS, hp, hh, tok],
                                        kst[l][0:SROWS, hp, tok], start=True, stop=True)
                    filled(ins, "s", f"S{l}{b}{c}", i)

            def turn_max(l, b, i):
                after(pe, f"nm{l}{b}", i)
                dst = fill(pe, "m", f"nmT{l}{b}", i)
                ins = pe.transpose(dst[:].bitcast(BF16)[:, 0:SEQ], nmw[:, b], identb[:])
                filled(ins, "m", f"nmT{l}{b}", i)

            def scores_turned(l, b, i):
                after(pe, f"max_in{b}", i, 16 * (l + 1), 32)
                for c in range(4):
                    dst = fill(pe, "t", f"T{l}{b}{c}", i)
                    tok = slice(b * SEQ, (b + 1) * SEQ)
                    for s in range(2):
                        hp = 2 * c + s
                        ins = pe.matmul(dst[:, 2 * s * SEQ:(2 * s + 2) * SEQ].rearrange("p (h q) -> p h q", h=2),
                                        kst[l][:, hp, tok], qz[l][:, hp, :, tok], start=True, stop=True)
                    filled(ins, "t", f"T{l}{b}{c}", i)

            def values(l, b, i):
                if l == 0 and b == 0:
                    after(pe, "va", i)
                dst = fill(pe, "m", f"C{l}{b}", i)
                for c in range(4):
                    if l:
                        freed(pe, "t", f"T1{b}{c}", i)
                    else:
                        after(pe, f"p0{b}", i, c + 1, 4)
                    for s in range(4 * c, 4 * c + 4):
                        head = HALF * (s % 2) + s // 2
                        j, g = head // 4, head % 4
                        ins = pe.matmul(dst[32 * j:32 * j + VW, g * SEQ:(g + 1) * SEQ], va[:, b, l, head],
                                        pt[:, b, s], start=True, stop=True)
                filled(ins, "m", f"C{l}{b}", i)

            def attention_out(l, i):
                after(pe, f"ct3{l}", i, of=2)
                dst = fill(pe, "m", f"o{l}", i)
                for b in range(2):
                    ins = pe.matmul(dst[:, b * D:(b + 1) * D], ct3[:, b], wo[:, l], start=True, stop=True)
                filled(ins, "m", f"o{l}", i)

            def ffn_up(n, i):
                if n == 0:
                    freed(pe, "m", "xn1T", i)
                dst = fill(pe, "m", f"ff{n}", i)
                for k in range(2):
                    f = 2 * n + k
                    ins = pe.matmul(dst[:, k * TOK:(k + 1) * TOK], w1[:, f * 128:(f + 1) * 128], xnT[1][:],
                                    start=True, stop=True)
                filled(ins, "m", f"ff{n}", i)

            def ffn_down(i):
                dst = fill(pe, "m", "ffy", i)
                for f in range(FCH):
                    if f % 2 == 0:
                        after(pe, "fh", i, f // 2 + 1, 2)
                    for b in range(2):
                        ins = pe.matmul(dst[:, b * D:(b + 1) * D], fh[:, f, b * SEQ:(b + 1) * SEQ], w2[:, f],
                                        start=(f == 0 and b == 0), stop=(f == FCH - 1), skip_group_check=True)
                filled(ins, "m", "ffy", i)

            def logits(turn):
                freed(pe, "m", "xn3T", turn)
                dst = fill(pe, "m", "logit", turn)
                for b in range(2):
                    ins = pe.matmul(dst[:, b * EXPERTS:(b + 1) * EXPERTS], xnT[3][:, b * SEQ:(b + 1) * SEQ], gateT[:],
                                    start=True, stop=True)
                filled(ins, "m", "logit", turn)

            def gate_up(c, turn):
                ring, name = ("s", f"gu{c}") if c < ECH else ("m", "shared")
                rows = 128 if c < ECH else HID
                dst = fill(pe, ring, name, turn)
                for k, w in enumerate((wg, wu)):
                    ins = pe.matmul(dst[0:rows, k * TOK:(k + 1) * TOK], w[:, c * 128:c * 128 + rows], xnT[3][:],
                                    start=True, stop=True)
                filled(ins, ring, name, turn)

            def turn_weights(p, turn):
                after(pe, "csp", p, of=3)
                dst = fill(pe, "m", "combT", turn)
                for b in range(2):
                    ins = pe.transpose(dst[:].bitcast(BF16)[:, b * SEQ:(b + 1) * SEQ], cspw[:, b], identb[:])
                filled(ins, "m", "combT", turn)
                freed(pe, "m", "combT", turn)

            def spread(c, turn):
                dst = fill(pe, "t", f"cb{c}", turn)
                filled(pe.matmul(dst[:, 0:TOK], expsel[:, c], combT[:], start=True, stop=True), "t", f"cb{c}", turn)

            def down(c, p, turn):
                rows = 128 if c < ECH else HID
                freed(pe, *(("t", f"cb{c}") if c < ECH else ("m", "shared")), turn)
                for b in range(2):
                    ins = pe.matmul(Y_BANK[:, b * D:(b + 1) * D], hT[0:rows, c % 2, b * SEQ:(b + 1) * SEQ],
                                    wd[:, c] if c < ECH else swd[:], start=(c == 0 and b == 0), stop=(c == ECH),
                                    skip_group_check=True)
                ins.then_inc(sem("down"), 1)

            def chunk(c, p, turn):
                if c + 2 <= ECH:
                    gate_up(c + 2, turn)
                    if c + 2 < ECH:
                        spread(c + 2, turn)
                down(c, p, turn)

            pe.wait_ge(sem("ffw_in"), 64)
            dst = fill(pe, "m", "w1", "setup")
            filled(pe.matmul(dst[:], u1t[:], v1[:], start=True, stop=True), "m", "w1", "setup")
            dst = fill(pe, "m", "w2", "setup")
            for n in range(FCH):
                ins = pe.matmul(dst[:, n * D:(n + 1) * D], u2t[:, n * 128:(n + 1) * 128], v2[:], start=True, stop=True)
            filled(ins, "m", "w2", "setup")
            pe.wait_ge(sem("rel_in"), 32)
            dst = fill(pe, "m", "rel0", "setup")
            ins = pe.matmul(dst[0:HEADS, 0:REL + 1], table[:], onehot[:], start=True, stop=True)
            filled(ins, "m", "rel0", "setup")
            pe.wait_ge(sem("ident_in"), 16)
            pe.wait_ge(sem("maskn"), 1)
            dst = fill(pe, "m", "maskT", "setup")
            filled(pe.transpose(dst[:, 0:SEQ], maskn[:], ident[:]), "m", "maskT", "setup")
            pe.wait_ge(sem("gate_normed"), 1)
            dst = fill(pe, "m", "gateT", "setup")
            filled(pe.transpose(dst[:, 0:EXPERTS], gsq[:], ident[0:EXPERTS, 0:EXPERTS]), "m", "gateT", "setup")
            turn_front(0, "setup")
            pe.wait_ge(sem("proj_in"), 32)
            keys("setup")
            queries(0, "setup")
            value_rows("setup")
            pe.wait_ge(sem("identb"), 1)
            pe.wait_ge(sem("wo_in"), 16)
            pe.wait_ge(sem("kst_ones"), 2)

            def body(i):
                p = i - 1
                first = isinstance(i, int) and i == 0
                last = isinstance(i, int) and i == PAIRS - 1
                scores(0, 0, i)
                if not first:
                    turn_tokens(3, "xn3T", p, i)
                    logits(i)
                scores(0, 1, i)
                turn_max(0, 0, i)
                if not first:
                    gate_up(0, i)
                turn_max(0, 1, i)
                scores_turned(0, 0, i)
                if not first:
                    gate_up(1, i)
                scores_turned(0, 1, i)
                values(0, 0, i)
                values(0, 1, i)
                if not first:
                    turn_weights(p, i)
                    spread(0, i)
                    spread(1, i)
                attention_out(0, i)
                if not first:
                    chunk(0, p, i)
                turn_tokens(1, "xn1T", i, i)
                if not last:
                    turn_front(i + 1, i)
                ffn_up(0, i)
                ffn_up(1, i)
                if not first:
                    chunk(1, p, i)
                if not last:
                    keys(i)
                    queries(0, i)
                if not first:
                    chunk(2, p, i)
                if not last:
                    value_rows(i)
                ffn_down(i)
                if not first:
                    chunk(3, p, i)
                turn_tokens(2, "xn2T", i, i)
                if not first:
                    chunk(4, p, i)
                queries(1, i)
                if not first:
                    for c in range(5, ECH + 1):
                        chunk(c, p, i)
                scores(1, 0, i)
                scores(1, 1, i)
                turn_max(1, 0, i)
                turn_max(1, 1, i)
                scores_turned(1, 0, i)
                scores_turned(1, 1, i)
                values(1, 0, i)
                values(1, 1, i)
                attention_out(1, i)

            body(0)
            pe.wait_ge(sem("moe_in"), 64)
            pe.wait_ge(sem("expsel"), 1)
            with pe.Fori(1, PAIRS - 1) as i:
                body(i)
            body(PAIRS - 1)
            p = PAIRS - 1
            turn_tokens(3, "xn3T", p, "tail")
            logits("tail")
            gate_up(0, "tail")
            gate_up(1, "tail")
            turn_weights(p, "tail")
            spread(0, "tail")
            spread(1, "tail")
            for c in range(ECH + 1):
                chunk(c, p, "tail")


def bucket_onehot():
    behind = np.maximum(np.arange(REL) - (SEQ - 1), 0)
    exact = BUCKETS // 2
    f = np.maximum(behind, 1).astype(np.float32)
    large = exact + (np.log(f / np.float32(exact)) / np.float32(np.log(MAX_DISTANCE / exact))
                     * np.float32(BUCKETS - exact)).astype(np.int32)
    bucket = np.where(behind < exact, behind, np.minimum(large, BUCKETS - 1))
    out = np.zeros((BUCKETS, REL + 1), np.float32)
    out[bucket, np.arange(REL)] = 1.0
    return out


def expert_selector():
    out = np.zeros((3, EXPERTS, ECH, 128), np.float32)
    for e in range(EXPERTS):
        first = e * HID
        out[:, e, first // 128, first % 128:first % 128 + HID] = 1.0
    return out.reshape(3 * EXPERTS, ECH, 128)


def kernel(**inputs):
    import numpy as _np
    import concourse.bacc as _bacc
    from concourse import mybir as _mybir
    from concourse.bass_utils import run_bass_kernel_spmd as _run

    a = {k: _np.asarray(v) for k, v in inputs.items()}
    heads_in = lambda w: w.transpose(1, 0, 2).reshape(D, D)
    wq1, wk1, wv1 = (heads_in(a[f"L1_xattn_W{c}"]) for c in "qkv")
    by_dim = lambda w: w.reshape(-1, 2, HALF, DK).swapaxes(2, 3).reshape(w.shape)
    experts_in = lambda w: w.transpose(1, 0, 2).reshape(D, EXPERTS * HID)
    arrays = {
        "x": a["x"],
        "ctx": a["ctx_1024"][:, ::-1],
        "mask": a["mask_1x1xSxS2_bk1"].reshape(SEQ, SEQ)[:, ::-1].view(_np.uint8),
        "wqk": _np.stack([_np.stack([by_dim(a["L0_xattn_Wq"]), by_dim(a["L0_xattn_Wk"])], 1),
                          _np.stack([by_dim(wq1), by_dim(wk1)], 1)], 1),
        "wv": _np.stack([a["L0_xattn_Wv"], wv1], 1),
        "wo": _np.stack([a["L0_xattn_Wo"], a["L1_xattn_Wo"]], 1),
        "bqk": _np.stack([by_dim(a[f"L{l}_xattn_b{c}"].reshape(D)) for l in range(2) for c in "qk"], 1),
        "bv": _np.tile(_np.concatenate([a["L0_xattn_bv"], a["L1_xattn_bv"].reshape(D)]), (2, 1)),
        "rows": _np.stack([_np.tile(a[n], (2, 1)) for n in ("L0_xattn_bo", "L0_ffn_b2", "L1_xattn_bo")]),
        "table": a["L0_xattn_rpe_table"],
        "u1t": a["L0_ffn_U1"].T,
        "v1": a["L0_ffn_V1"],
        "b1": a["L0_ffn_b1"].reshape(FCH, 128).T,
        "u2t": a["L0_ffn_U2"].T,
        "v2": a["L0_ffn_V2"],
        "gate": a["L1_ffn_gate_w"],
        "wg": _np.concatenate([experts_in(a["L1_ffn_w_gate"]), a["L1_ffn_sw_gate"]], 1),
        "wu": _np.concatenate([experts_in(a["L1_ffn_w_up"]), a["L1_ffn_sw_up"]], 1),
        "wd": a["L1_ffn_w_down"].reshape(ECH, 128, D).transpose(1, 0, 2),
        "swd": a["L1_ffn_sw_down"],
        "ident": _np.eye(128, dtype=_np.float32),
        "onehot": bucket_onehot(),
        "expsel": expert_selector(),
    }
    arrays = {f"in_{k}": _np.ascontiguousarray(v) for k, v in arrays.items()}
    nc = _bacc.Bacc("TRN2", target_bir_lowering=False, num_devices=1)
    args = [nc.dram_tensor(k, v.shape, _mybir.dt.from_np(v.dtype), kind="ExternalInput").ap() for k, v in arrays.items()]
    args.append(nc.dram_tensor("out_0", (BATCH, SEQ, D), _mybir.dt.float32, kind="ExternalOutput").ap())
    bass_xattn_ffn_moe(nc, *args)
    r = _run(nc, [arrays], core_ids=[0])
    return r.results[0]["out_0"]
```

```python
from contextlib import ExitStack

import numpy as np

import concourse.bass as bass
from concourse import mybir

F32 = mybir.dt.float32
BF16 = mybir.dt.bfloat16
U8 = mybir.dt.uint8
ACT = mybir.ActivationFunctionType
ALU = mybir.AluOpType
AX = mybir.AxisListType

BATCH, SEQ, D = 8, 128, 128
HEADS, DK = 16, 8
HALF = HEADS // 2
PAIRS = BATCH // 2
TOK = 2 * SEQ
FF, RANK = 512, 32
FCH = FF // 128
EXPERTS, HID, TOPK = 16, 64, 8
ECH = EXPERTS * HID // 128
BUCKETS, MAX_DISTANCE = 32, 512
REL = 2 * SEQ - 1
MASKED = float(2 ** 100)
LN_EPS, L2_EPS = 1e-5, 1e-12
GELU_C, GELU_A = 0.7978845608028654, 0.044715
SCALE = float(DK) ** -0.5

Q_PART = (0, 0, 0, 1, 1, 2)
K_PART = (0, 1, 2, 0, 1, 0)
PRODS = len(Q_PART)
HROWS = PRODS * DK
SROWS = 2 * HROWS
MROWS = SROWS + 6
VW = 32


def bass_xattn_ffn_moe(nc, x_d, ctx_d, mask_d, wqk_d, wv_d, wo_d, bqk_d, bv_d, rows_d, table_d, u1t_d, v1_d, b1_d,
                       u2t_d, v2_d, gate_d, wg_d, wu_d, wd_d, swd_d, ident_d, onehot_d, expsel_d, out_d):
    rel_d = nc.dram_tensor("rel_bias_scratch", (HEADS, REL + 1), F32, kind="Internal").ap()

    with ExitStack() as ctx:
        def sb(name, shape, dt=F32):
            return ctx.enter_context(nc.sbuf_tensor(name, shape, dt))

        sems = {}

        def sem(name):
            if name not in sems:
                sems[name] = ctx.enter_context(nc.semaphore(name))
            return sems[name]

        def after(eng, name, p, n=None, of=1):
            n = of if n is None else n
            v = p * of + n
            if not (isinstance(v, int) and v <= 0):
                eng.wait_ge(sem(name), v)

        def before(eng, name, p, of=1):
            if not (isinstance(p, int) and p == 0):
                eng.wait_ge(sem(name), p * of)

        bank = [ctx.enter_context(nc.psum_tensor(f"bank{i}", [128, 512], F32)) for i in range(8)]
        Y_BANK = bank[7]

        FRONT = ["xcT", "k0", "k1", "q0", "v0", "v1"]
        LATE = (["xn3T", "logit", "combT", "shared", "C10", "C11", "nmT10", "nmT11", "o1"]
                + [f"{n}{c}" for n in ("gu", "cb") for c in range(ECH)]
                + [f"{n}1{b}{c}" for n in "ST" for b in range(2) for c in range(4)])
        BODY = {
            "m": ["xcT", "nmT10", "k0", "k1", "q0", "nmT11", "C10", "C11", "o1", "C00", "C01", "xn3T",
                  "logit", "o0", "v0", "v1", "xn1T", "ff0", "ff1", "combT", "ffy", "xn2T", "q1", "shared"],
            "s": [f"S{lb}{c}" for lb in ("00", "10", "11", "01") for c in range(4)] + [f"gu{c}" for c in range(ECH)],
            "t": [f"T{lb}{c}" for lb in ("00", "10", "11", "01") for c in range(4)] + [f"cb{c}" for c in range(ECH)],
        }
        BANKS = {"m": bank[4:7], "s": bank[0:2], "t": bank[2:4]}
        SETUP = {"m": ["xcT", "rel0", "k0", "k1", "q0", "v0", "v1", "w1", "w2", "gateT"], "s": [], "t": []}

        def uses(ring, turn):
            if isinstance(turn, str) and turn == "setup":
                return SETUP[ring]
            if isinstance(turn, str):
                return [u for u in BODY[ring] if u in LATE]
            skip = []
            if isinstance(turn, int) and turn == 0:
                skip = LATE
            elif isinstance(turn, int) and turn == PAIRS - 1:
                skip = FRONT
            names = [u for u in BODY[ring] if u not in skip]
            if ring == "m" and isinstance(turn, int) and turn == 0:
                names.remove("C00")
                names.remove("C01")
                names[0:1] = ["C00", "xcT", "C01"]
            return names

        def number(ring, name, turn):
            k, body = len(BANKS[ring]), BODY[ring]
            assert len(body) % k == 0
            n = uses(ring, turn).index(name)
            if isinstance(turn, str) and turn == "setup":
                return n % k, n // k
            if isinstance(turn, int) and turn == 0:
                n += len(SETUP[ring])
                return n % k, n // k
            n += len(SETUP[ring]) + len(uses(ring, 0))
            if isinstance(turn, str):
                n += len(body) * (PAIRS - 2) + len(uses(ring, PAIRS - 1))
                return n % k, n // k
            return n % k, turn * (len(body) // k) + (n // k - len(body) // k)

        def fill(pe, ring, name, turn):
            k, n = number(ring, name, turn)
            if not (isinstance(n, int) and n == 0):
                pe.wait_ge(sem(f"{ring}_free{k}"), n)
            return BANKS[ring][k]

        def filled(ins, ring, name, turn):
            ins.then_inc(sem(f"{ring}_full{number(ring, name, turn)[0]}"), 1)

        def read(eng, ring, name, turn):
            k, n = number(ring, name, turn)
            eng.wait_ge(sem(f"{ring}_full{k}"), n + 1)
            return BANKS[ring][k]

        def free(ins, ring, name, turn):
            ins.then_inc(sem(f"{ring}_free{number(ring, name, turn)[0]}"), 1)

        def freed(eng, ring, name, turn):
            k, n = number(ring, name, turn)
            eng.wait_ge(sem(f"{ring}_free{k}"), n + 1)

        wqk = sb("wqk", [128, 2, 2, D])
        wv = sb("wv", [128, 2, D])
        wo = sb("wo", [128, 2, D])
        bqk = sb("bqk", [128, 4])
        bqs = sb("bqs", [128, 2])
        bvb = sb("bvb", [128, 2, 2 * D])
        rowb = sb("rowb", [128, 3, 2, D])
        table = sb("table", [BUCKETS, HEADS])
        onehot = sb("onehot", [BUCKETS, REL + 1])
        u1t = sb("u1t", [RANK, D])
        v1 = sb("v1", [RANK, FF])
        b1 = sb("b1", [128, FCH])
        u2t = sb("u2t", [RANK, FF])
        v2 = sb("v2", [RANK, D])
        w1 = sb("w1", [128, FF])
        w2 = sb("w2", [128, FCH, D])
        gate = sb("gate", [EXPERTS, D])
        gsq = sb("gsq", [EXPERTS, D])
        gss = sb("gss", [EXPERTS, 2])
        gateT = sb("gateT", [128, EXPERTS])
        wg = sb("wg", [128, EXPERTS * HID + HID])
        wu = sb("wu", [128, EXPERTS * HID + HID])
        wd = sb("wd", [128, ECH, D])
        swd = sb("swd", [HID, D])
        ident = sb("ident", [128, 128])
        identb = sb("identb", [128, 128], BF16)
        expsel = sb("expsel", [3 * EXPERTS, ECH, 128], BF16)
        mask8 = sb("mask8", [SEQ, SEQ], U8)
        maskn = sb("maskn", [SEQ, SEQ])
        relrow = sb("relrow", [HEADS, REL + 1])
        biasq = sb("biasq", [SEQ, HALF, 2, SEQ])
        half = sb("half", [128, 4])

        x0 = sb("x0", [128, 2, D])
        cx = sb("cx", [128, 2, D])
        res = [sb(f"res{n}", [128, 2, D]) for n in range(4)]
        xs = [None] + [sb(f"x{n}", [128, 2, D]) for n in range(1, 4)]
        xout = sb("xout", [128, 2, D])
        xn = [sb(f"xn{n}", [128, 2, D]) for n in range(4)]
        xnT = [sb(f"xnT{n}", [128, TOK]) for n in range(4)]
        xcT = sb("xcT_sb", [128, 2, TOK])
        stats = sb("stats", [128, 4, 2, 6])
        mv = sb("mv", [128, 4, 2, 2])
        ve = sb("ve", [128, 4, 2])
        rstd = sb("rstd", [128, 4, 2])
        tiny = sb("tiny", [128, 4])
        qf = sb("qf", [128, 2, TOK])
        qr = sb("qr", [128, 2, TOK])
        qsp = sb("qsp", [128, 3, 2, TOK], BF16)
        kf = sb("kf", [128, 2, TOK])
        kr = sb("kr", [128, 2, TOK])
        ksp = sb("ksp", [128, 3, 2, TOK], BF16)
        qst = [sb("qst0", [SROWS, HALF, 2, TOK], BF16), sb("qst1", [MROWS, HALF, TOK], BF16)]
        kst = [sb("kst0", [SROWS, HALF, TOK], BF16), sb("kst1", [MROWS, HALF, 2, TOK], BF16)]
        STACK_DMAS = {"qst0": 2 * PRODS, "kst0": PRODS, "qst1": PRODS, "kst1": 2 * PRODS}
        ones = sb("ones", [3, HALF, TOK], BF16)
        vf = sb("vf", [128, 2 * TOK])
        va = sb("va", [128, 2, 2, HEADS, VW])
        es = sb("es", [128, 2, HEADS, SEQ])
        mx = sb("mx", [128, 2, 2, HEADS])
        mr = sb("mr", [128, 2, HEADS])
        nmw = sb("nm", [128, 2, 128], BF16)
        nm = nmw[:, :, 0:3 * HEADS].rearrange("p b (hh n hp) -> p b n hp hh", hh=2, n=3)
        nmT = sb("nmT_sb", [3 * HEADS, 2, SEQ], BF16)
        pt = sb("pt", [128, 2, 2, HEADS, SEQ])
        ct1 = sb("ct1", [128, 2, 4, 4, 32])
        crc = sb("crc", [128, 2, 4, 4])
        ct2 = sb("ct2", [128, 2, 4, 4, DK])
        ct3 = sb("ct3", [128, 2, 2, SEQ])
        fv = sb("fv", [128, FCH, TOK])
        fs = sb("fs", [128, FCH, TOK])
        fw = sb("fw", [128, FCH, TOK])
        fh = sb("fh", [128, FCH, TOK])
        expself = fw[0:3 * EXPERTS].rearrange("p a t -> p (a t)").rearrange("p (c u) -> p c u", c=ECH)
        sq = sb("sq", [128, 2, D])
        ss = sb("ss", [128, 2])
        sc = sb("sc", [128, 2])
        rn = sb("rn", [128, 2])
        lg = sb("lg", [128, 2, EXPERTS])
        top = sb("top", [128, 2, TOPK])
        lr = sb("lr", [128, 2, EXPERTS])
        sel = sb("sel", [128, 2, EXPERTS])
        th = sb("th", [128, 2, EXPERTS])
        sw = sb("sw", [128, 2, EXPERTS])
        sws = sb("sws", [128, 2])
        swr = sb("swr", [128, 2])
        comb = sb("comb", [128, 2, EXPERTS])
        cr = sb("cr", [128, 2, EXPERTS])
        cspw = sb("csp", [128, 2, 128], BF16)
        csp = cspw[:, :, 0:3 * EXPERTS].rearrange("p b (n e) -> p b n e", n=3)
        combT = sb("combT_sb", [3 * EXPERTS, TOK], BF16)
        gth = sb("gth", [128, 4, TOK])
        ga = sb("ga", [128, 2, TOK])
        gb = sb("gb", [128, 4, TOK])
        hT = sb("hT", [128, 2, TOK])

        block = ctx.enter_context(nc.Block())

        def load_pair(eng, p):
            eng.dma_start(x0[:], x_d[bass.ds(2 * p, 2)].rearrange("b s d -> s b d")).then_inc(sem("x0_in"), 16)
            eng.dma_start(cx[:], ctx_d[bass.ds(2 * p, 2)].rearrange("b s d -> s b d")).then_inc(sem("cx_in"), 16)

        @block.sync
        def _(sp):
            def stack(to, name, parts, l, n, part):
                r = 2 * DK * n
                if STACK_DMAS[f"{name}{l}"] == PRODS:
                    sp.dma_start(to[l][r:r + 2 * DK, :, :], parts[:, part, l, :]).then_inc(sem(f"{name}{l}_in"), 16)
                else:
                    for hh in range(2):
                        sp.dma_start(to[l][r + DK * hh:r + DK * hh + DK, :, hh, :],
                                     parts[64 * hh:64 * hh + 64, part, l, :]).then_inc(sem(f"{name}{l}_in"), 16)

            def stack_q(l, p, turn):
                for n, part in enumerate(Q_PART):
                    if n == Q_PART.index(part):
                        if part == 0:
                            freed(sp, "m", f"q{l}", turn)
                        else:
                            after(sp, f"q_{('mid', 'split')[part - 1]}{l}", p)
                    stack(qst, "qst", qsp, l, n, part)

            def stack_k(l, p, turn):
                for part in range(3):
                    if l == 0 or isinstance(turn, str):
                        if l == 1:
                            after(sp, "k_split1", p)
                        elif part == 0:
                            freed(sp, "m", "k0", turn)
                        else:
                            after(sp, f"k_{('mid', 'split')[part - 1]}0", p)
                    for n in range(PRODS):
                        if K_PART[n] == part:
                            stack(kst, "kst", ksp, l, n, part)

            def max_rows(b, turn):
                freed(sp, "m", f"nmT1{b}", turn)
                sp.dma_start(qst[1][SROWS:MROWS, :, b * SEQ:(b + 1) * SEQ],
                             nmT[:, b, :]).then_inc(sem(f"max1{b}_in"), 16)

            load_pair(sp, 0)
            sp.dma_start(ident[:], ident_d).then_inc(sem("ident_in"), 16)
            sp.dma_start(wqk[:], wqk_d).then_inc(sem("wqk_in"), 16)
            sp.dma_start(bqk[:], bqk_d).then_inc(sem("bqk_in"), 16)
            sp.dma_start(table[:], table_d).then_inc(sem("rel_in"), 16)
            sp.dma_start(onehot[:], onehot_d).then_inc(sem("rel_in"), 16)
            sp.dma_start(wv[:], wv_d).then_inc(sem("wv_in"), 16)
            sp.dma_start(mask8[:], mask_d).then_inc(sem("mask_in"), 16)
            sp.dma_start(gate[:], gate_d).then_inc(sem("gate_in"), 16)
            sp.dma_start(bvb[:], bv_d.partition_broadcast(128)).then_inc(sem("bias_in"), 16)
            sp.dma_start(rowb[:], rows_d.partition_broadcast(128)).then_inc(sem("bias_in"), 16)
            sp.dma_start(u1t[:], u1t_d).then_inc(sem("ffw_in"), 16)
            sp.dma_start(v1[:], v1_d).then_inc(sem("ffw_in"), 16)
            freed(sp, "m", "rel0", "setup")
            sp.dma_start(rel_d, relrow[:]).then_inc(sem("stored"), 16)
            sp.dma_start(u2t[:], u2t_d).then_inc(sem("ffw_in"), 16)
            sp.dma_start(v2[:], v2_d).then_inc(sem("ffw_in"), 16)
            sp.dma_start(b1[:], b1_d).then_inc(sem("b1_in"), 16)
            sp.wait_ge(sem("stored"), 16)
            for hh in range(2):
                src = bass.AP(tensor=rel_d.tensor, offset=HALF * hh * (REL + 1),
                              ap=[[1, SEQ], [REL + 1, HALF], [1, SEQ]])
                sp.dma_start(biasq[:, :, hh, :], src).then_inc(sem("biasq_in"), 16)
            stack_k(0, 0, "setup")
            sp.wait_ge(sem("stacks_cleared"), 2)
            stack_q(0, 0, "setup")
            after(sp, "res0", 0)
            load_pair(sp, 1)
            sp.wait_ge(sem("ones"), 1)
            for hh in range(2):
                r = SROWS + 3 * hh
                sp.dma_start(kst[1][r:r + 3, :, hh, :], ones[:]).then_inc(sem("kst_ones"), 16)
            after(sp, "k_split1", 0)

            def store(p, first):
                after(sp, "xout", p, of=2)
                sp.dma_start(out_d[bass.ds(first, 2)].rearrange("b s d -> s b d"), xout[:]).then_inc(sem("stored"), 16)

            def body(i):
                first = isinstance(i, int) and i == 0
                last = isinstance(i, int) and i == PAIRS - 1
                out_row = 2 * (i - 1) if isinstance(i, int) else sp.snap(2 * i - 2)
                if first:
                    sp.dma_start(wo[:], wo_d).then_inc(sem("wo_in"), 16)
                    sp.dma_start(expself[:], expsel_d).then_inc(sem("expsel_in"), 16)
                    sp.dma_start(wg[:], wg_d).then_inc(sem("moe_in"), 16)
                    sp.dma_start(wu[:], wu_d).then_inc(sem("moe_in"), 16)
                    sp.dma_start(wd[:], wd_d).then_inc(sem("moe_in"), 16)
                    sp.dma_start(swd[:], swd_d).then_inc(sem("moe_in"), 16)
                if not first:
                    max_rows(0, i)
                    max_rows(1, i)
                    read(sp, "t", "T113", i)
                else:
                    read(sp, "s", "S013", i)
                stack_k(1, i, i)
                if not last:
                    stack_k(0, i + 1, i)
                    stack_q(0, i + 1, i)
                stack_q(1, i, i)
                if not first:
                    store(i - 1, out_row)

            body(0)
            with sp.Fori(1, PAIRS - 1) as i:
                body(i)
            body(PAIRS - 1)
            max_rows(0, "tail")
            max_rows(1, "tail")
            store(PAIRS - 1, 2 * (PAIRS - 1))
            sp.wait_ge(sem("stored"), 16 * (PAIRS + 1))

        @block.gpsimd
        def _(pool):
            def power(n, p):
                after(pool, f"ve{n}", p)
                pool.tensor_tensor(rstd[:, n, :], ve[:, n, :], half[:, 0:2], ALU.pow).then_inc(sem(f"rstd{n}"), 1)

            def residual(n, src):
                pool.tensor_tensor(res[n][:], src[:], rowb[:, n], ALU.add).then_inc(sem(f"res{n}"), 1)

            def rest_q(l, p, turn):
                freed(pool, "m", f"q{l}", turn)
                pool.tensor_tensor(qr[:, l], qf[:, l], qsp[:, 0, l], ALU.subtract).then_inc(sem(f"q_rest{l}"), 1)

            def last_q(l, p):
                after(pool, f"q_mid{l}", p)
                pool.tensor_tensor(qsp[:, 2, l], qr[:, l], qsp[:, 1, l], ALU.subtract).then_inc(sem(f"q_split{l}"), 1)

            def rest_k(l, p, turn):
                if l == 0:
                    freed(pool, "m", "k0", turn)
                else:
                    after(pool, "k_top1", p)
                pool.tensor_tensor(kr[:, l], kf[:, l], ksp[:, 0, l], ALU.subtract).then_inc(sem(f"k_rest{l}"), 1)

            def last_k(l, p):
                after(pool, f"k_mid{l}", p)
                pool.tensor_tensor(ksp[:, 2, l], kr[:, l], ksp[:, 1, l], ALU.subtract).then_inc(sem(f"k_split{l}"), 1)

            def add_value_bias(l, p, turn):
                if l == 0:
                    freed(pool, "m", "v1", turn)
                elif not (isinstance(turn, int) and turn == 0):
                    read(pool, "m", "C11", turn)
                pool.tensor_tensor(va[:, l, :, :, 0:DK],
                                   vf[:].rearrange("p (b l h d) -> p b l h d", b=2, l=2, d=DK)[:, :, l],
                                   bvb[:].rearrange("p b (l h d) -> p b l h d", l=2, d=DK)[:, :, l],
                                   ALU.add).then_inc(sem(f"va{l}"), 1)

            def less_least(b, i):
                for c in range(4):
                    h = slice(4 * c, 4 * c + 4)
                    after(pool, f"mx0{b}", i, c + 1, 4)
                    pool.tensor_tensor(es[:, b, h], es[:, b, h], mx[:, 0, b, h].unsqueeze(2).broadcast_to([128, 4, SEQ]),
                                       ALU.subtract).then_inc(sem(f"less0{b}"), 1)

            def router_norm(p):
                after(pool, "ss_clamped", p)
                pool.tensor_tensor(rn[:], sc[:], half[:, 0:2], ALU.pow).then_inc(sem("rn"), 1)

            pool.memset(half[:], -0.5).then_inc(sem("half"), 1)
            pool.wait_ge(sem("half"), 1)
            power(0, 0)
            rest_k(0, 0, "setup")
            rest_q(0, 0, "setup")
            last_k(0, 0)
            last_q(0, 0)
            rest_k(1, 0, "setup")
            last_k(1, 0)
            pool.wait_ge(sem("gss"), 1)
            pool.tensor_tensor(gss[:, 1:2], gss[:, 0:1], half[0:EXPERTS, 0:1], ALU.pow).then_inc(sem("gate_norm"), 1)
            pool.wait_ge(sem("bias_in"), 32)
            after(pool, "x0_in", 0, of=16)
            residual(0, x0)
            pool.wait_ge(sem("va_cleared"), 1)
            add_value_bias(0, 0, "setup")

            def body(i):
                first = isinstance(i, int) and i == 0
                last = isinstance(i, int) and i == PAIRS - 1
                p = i - 1
                less_least(0, i)
                if not last:
                    power(0, i + 1)
                if first:
                    less_least(1, i)
                    add_value_bias(1, i, i)
                if not last:
                    rest_k(0, i + 1, i)
                    rest_q(0, i + 1, i)
                if not first:
                    less_least(1, i)
                if not last:
                    last_k(0, i + 1)
                    last_q(0, i + 1)
                if not first:
                    add_value_bias(1, i, i)
                if not first:
                    power(3, p)
                if not first:
                    router_norm(p)
                power(1, i)
                residual(1, xs[1])
                if not last:
                    residual(0, x0)
                    rest_k(1, i + 1, i)
                    last_k(1, i + 1)
                    add_value_bias(0, i + 1, i)
                power(2, i)
                residual(2, xs[2])
                rest_q(1, i, i)
                last_q(1, i)

            body(0)
            with pool.Fori(1, PAIRS - 1) as i:
                body(i)
            body(PAIRS - 1)
            power(3, PAIRS - 1)
            router_norm(PAIRS - 1)

        @block.scalar
        def _(act):
            def copy_turned(dst, name, turn):
                src = read(act, "m", name, turn)
                free(act.activation(dst, src[:, 0:TOK], ACT.Copy), "m", name, turn)

            def copy_front(turn):
                src = read(act, "m", "xcT", turn)
                free(act.activation(xcT[:], src[:], ACT.Copy), "m", "xcT", turn)

            def project_q(l, p, turn):
                src = read(act, "m", f"q{l}", turn)[:, 0:TOK]
                before(act, f"qst{l}_in", p, of=16 * STACK_DMAS[f"qst{l}"])
                scale = SCALE if l else -SCALE
                act.activation(qf[:, l], src, ACT.Identity, bias=bqs[:, l:l + 1], scale=scale)
                free(act.activation(qsp[:, 0, l], src, ACT.Identity, bias=bqs[:, l:l + 1], scale=scale),
                     "m", f"q{l}", turn)

            def middle_q(l, p):
                after(act, f"q_rest{l}", p)
                act.activation(qsp[:, 1, l], qr[:, l], ACT.Copy).then_inc(sem(f"q_mid{l}"), 1)

            def project_k(l, p, turn):
                src = read(act, "m", f"k{l}", turn)[:, 0:TOK]
                bias = bqk[:, 2 * l + 1:2 * l + 2]
                if l == 0:
                    before(act, "kst0_in", p, of=16 * STACK_DMAS["kst0"])
                    act.activation(ksp[:, 0, 0], src, ACT.Identity, bias=bias)
                free(act.activation(kf[:, l], src, ACT.Identity, bias=bias), "m", f"k{l}", turn)

            def top_k1(p, turn):
                before(act, "kst1_in", p, of=16 * STACK_DMAS["kst1"])
                freed(act, "m", "k1", turn)
                act.activation(ksp[:, 0, 1], kf[:, 1], ACT.Copy).then_inc(sem("k_top1"), 1)

            def middle_k(l, p):
                after(act, f"k_rest{l}", p)
                act.activation(ksp[:, 1, l], kr[:, l], ACT.Copy).then_inc(sem(f"k_mid{l}"), 1)

            def copy_v(b, p, turn):
                src = read(act, "m", f"v{b}", turn)
                if b == 0:
                    before(act, "va1", p)
                free(act.activation(vf[:, b * TOK:(b + 1) * TOK], src[:, 0:TOK], ACT.Copy), "m", f"v{b}", turn)

            def max_turned(b, turn):
                src = read(act, "m", f"nmT1{b}", turn)
                v = src[:].bitcast(BF16)[0:3 * HEADS, 0:SEQ]
                free(act.activation(nmT[:, b], v, ACT.Copy), "m", f"nmT1{b}", turn)

            def weights(b, c, i):
                after(act, f"less0{b}", i, c + 1, 4)
                h = slice(4 * c, 4 * c + 4)
                act.activation(es[:, b, h], es[:, b, h], ACT.Exp, scale=-1.0).then_inc(sem(f"p0{b}"), 1)

            def copy_weights(b, c, i):
                src = read(act, "t", f"T0{b}{c}", i)
                free(act.activation(pt[:, 0, b, 4 * c:4 * c + 4, :], src[:], ACT.Copy), "t", f"T0{b}{c}", i)

            def softmax1(b, turn):
                for c in range(4):
                    src = read(act, "t", f"T1{b}{c}", turn)
                    free(act.activation(pt[:, 1, b, 4 * c:4 * c + 4, :], src[:], ACT.Exp), "t", f"T1{b}{c}", turn)

            def gelu_input(n, i):
                src = read(act, "m", f"ff{n}", i)
                for k in range(2):
                    f = 2 * n + k
                    ins = act.activation(fv[:, f], src[:, k * TOK:(k + 1) * TOK], ACT.Identity, bias=b1[:, f:f + 1])
                free(ins, "m", f"ff{n}", i)
                freed(act, "m", f"ff{n}", i)
                act.activation(fs[:, 2 * n:2 * n + 2], fv[:, 2 * n:2 * n + 2], ACT.Square, scale=GELU_A ** 0.5)\
                   .then_inc(sem("fsq"), 1)

            def gelu_tanh(n, i):
                after(act, "fw", i, n + 1, 2)
                act.activation(fs[:, 2 * n:2 * n + 2], fw[:, 2 * n:2 * n + 2], ACT.Tanh, scale=GELU_C)\
                   .then_inc(sem("ftanh"), 1)

            def router_squares(p):
                after(act, "xn3", p, of=2)
                for b in range(2):
                    act.activation(sq[:, b], xn[3][:, b], ACT.Square, accum_out=ss[:, b:b + 1]).then_inc(sem("ss"), 1)

            def router_tanh(p, turn):
                freed(act, "m", "logit", turn)
                act.activation(th[:], lg[:], ACT.Tanh, scale=0.5).then_inc(sem("th"), 1)

            def copy_comb(turn):
                src = read(act, "m", "combT", turn)
                v = src[:].bitcast(BF16)[0:3 * EXPERTS, 0:TOK]
                free(act.activation(combT[:], v, ACT.Copy), "m", "combT", turn)

            def gate_tanh(c, p, turn):
                if c >= 4:
                    after(act, "ga", p, c - 3, ECH + 1)
                if c < ECH:
                    src, rows = read(act, "s", f"gu{c}", turn), 128
                else:
                    src, rows = read(act, "m", "shared", turn), HID
                act.activation(gth[0:rows, c % 4], src[0:rows, 0:TOK], ACT.Tanh, scale=0.5).then_inc(sem("gth"), 1)

            act.wait_ge(sem("bqk_in"), 16)
            act.activation(bqs[:, 0:1], bqk[:, 0:1], ACT.Copy, scale=-SCALE)
            act.activation(bqs[:, 1:2], bqk[:, 2:3], ACT.Copy, scale=SCALE).then_inc(sem("bqs"), 1)
            act.wait_ge(sem("bqs"), 1)
            copy_front("setup")
            project_k(0, 0, "setup")
            project_k(1, 0, "setup")
            project_q(0, 0, "setup")
            middle_k(0, 0)
            middle_q(0, 0)
            top_k1(0, "setup")
            middle_k(1, 0)
            act.wait_ge(sem("gate_in"), 16)
            act.activation(gsq[:], gate[:], ACT.Square, accum_out=gss[:, 0:1]).then_inc(sem("gsq"), 1)
            copy_v(0, 0, "setup")
            copy_v(1, 0, "setup")
            act.wait_ge(sem("b1_in"), 16)

            def body(i):
                p = i - 1
                first = isinstance(i, int) and i == 0
                last = isinstance(i, int) and i == PAIRS - 1
                if not first and not last:
                    load_pair(act, i + 1)
                weights(0, 0, i)
                for c in range(1, 4):
                    weights(0, c, i)
                    copy_weights(0, c - 1, i)
                copy_weights(0, 3, i)
                if first:
                    for c in range(4):
                        weights(1, c, i)
                        if c > 0:
                            copy_weights(1, c - 1, i)
                    copy_weights(1, 3, i)
                if not last:
                    copy_front(i)
                if not first:
                    max_turned(0, i)
                if not last:
                    project_k(0, i + 1, i)
                    project_k(1, i + 1, i)
                    project_q(0, i + 1, i)
                if not first:
                    max_turned(1, i)
                    softmax1(0, i)
                if not last:
                    middle_k(0, i + 1)
                    middle_q(0, i + 1)
                if not first:
                    softmax1(1, i)
                    for c in range(4):
                        weights(1, c, i)
                    for c in range(4):
                        copy_weights(1, c, i)
                if not first:
                    router_squares(p)
                    copy_turned(xnT[3][:], "xn3T", i)
                if not last:
                    copy_v(0, i + 1, i)
                if not first:
                    router_tanh(p, i)
                    gate_tanh(0, p, i)
                    gate_tanh(1, p, i)
                if not last:
                    copy_v(1, i + 1, i)
                copy_turned(xnT[1][:], "xn1T", i)
                if not last:
                    top_k1(i + 1, i)
                gelu_input(0, i)
                gelu_input(1, i)
                if not first:
                    copy_comb(i)
                if not last:
                    middle_k(1, i + 1)
                gelu_tanh(0, i)
                gelu_tanh(1, i)
                if not first:
                    for c in range(2, 6):
                        gate_tanh(c, p, i)
                copy_turned(xnT[2][:], "xn2T", i)
                project_q(1, i, i)
                if not first:
                    gate_tanh(6, p, i)
                middle_q(1, i)
                if not first:
                    for c in range(7, ECH + 1):
                        gate_tanh(c, p, i)

            body(0)
            with act.Fori(1, PAIRS - 1) as i:
                body(i)
            body(PAIRS - 1)
            p = PAIRS - 1
            for b in range(2):
                max_turned(b, "tail")
                softmax1(b, "tail")
            router_squares(p)
            copy_turned(xnT[3][:], "xn3T", "tail")
            router_tanh(p, "tail")
            gate_tanh(0, p, "tail")
            gate_tanh(1, p, "tail")
            copy_comb("tail")
            for c in range(2, ECH + 1):
                gate_tanh(c, p, "tail")

        @block.vector
        def _(dve):
            def variance(n, src, p):
                for b in range(2):
                    dve.bn_stats(stats[:, n, b], src[:, b]).then_inc(sem(f"stats{n}"), 1)
                after(dve, f"stats{n}", p, of=2)
                dve.tensor_copy(tiny[:, 1:2], half[:, 0:1]).then_inc(sem("wait_carried"), 1)
                for b in range(2):
                    dve.bn_aggr(mv[:, n, b], stats[:, n, b]).then_inc(sem(f"mv{n}"), 1)
                after(dve, f"mv{n}", p, of=2)
                dve.tensor_scalar(ve[:, n], mv[:, n, :, 1], LN_EPS, None, ALU.add).then_inc(sem(f"ve{n}"), 1)

            def normalize(n, src, p):
                after(dve, f"rstd{n}", p)
                for b in range(2):
                    dve.tensor_scalar(xn[n][:, b], src[:, b], mv[:, n, b, 0:1], rstd[:, n, b:b + 1],
                                      ALU.subtract, ALU.mult).then_inc(sem(f"xn{n}"), 1)

            def row_max0(b, i):
                def least(c):
                    freed(dve, "s", f"S0{b}{c}", i)
                    dve.tensor_reduce(mx[:, 0, b, 4 * c:4 * c + 4], es[:, b, 4 * c:4 * c + 4], AX.X, ALU.min)\
                       .then_inc(sem(f"mx0{b}"), 1)

                for c in range(4):
                    src = read(dve, "s", f"S0{b}{c}", i)
                    free(dve.tensor_tensor(es[:, b, 4 * c:4 * c + 4], src[:].rearrange("p (h k) -> p h k", h=4),
                                           biasq[:, 2 * c:2 * c + 2].rearrange("p a b k -> p (a b) k"), ALU.add),
                         "s", f"S0{b}{c}", i)
                    if c:
                        least(c - 1)
                least(3)

            def row_max1(b, p, turn):
                for c in range(4):
                    src = read(dve, "s", f"S1{b}{c}", turn)
                    free(dve.tensor_reduce(mx[:, 1, b, 4 * c:4 * c + 4], src[:].rearrange("p (h k) -> p h k", h=4),
                                           AX.X, ALU.max), "s", f"S1{b}{c}", turn)
                for c in (2, 3):
                    freed(dve, "s", f"S1{b}{c}", turn)
                to = nm[:, b]
                src, rest = (t.rearrange("p (hp hh) -> p hp hh", hh=2) for t in (mx[:, 1, b], mr[:, b]))
                dve.tensor_scalar(to[:, 0], src, -1.0, None, ALU.mult).then_inc(sem("nm_a"), 1)
                after(dve, "nm_a", p, b + 1, 2)
                dve.scalar_tensor_tensor(rest, src, -1.0, to[:, 0], ALU.mult, ALU.subtract).then_inc(sem("nm_b"), 1)
                after(dve, "nm_b", p, b + 1, 2)
                dve.tensor_copy(to[:, 1], rest).then_inc(sem("nm_c"), 1)
                after(dve, "nm_c", p, b + 1, 2)
                dve.tensor_tensor(to[:, 2], rest, to[:, 1], ALU.subtract).then_inc(sem(f"nm1{b}"), 1)

            def context(l, p, turn):
                for b in range(2):
                    src = read(dve, "m", f"C{l}{b}", turn)
                    free(dve.transpose(ct1[:, b], src[:]), "m", f"C{l}{b}", turn)
                for b in range(2):
                    freed(dve, "m", f"C{l}{b}", turn)
                    dve.reciprocal(crc[:, b], ct1[:, b, :, :, DK]).then_inc(sem(f"crc{l}"), 1)
                for b in range(2):
                    after(dve, f"crc{l}", p, b + 1, 2)
                    dve.tensor_tensor(ct2[:, b].rearrange("p q g d -> p g q d"), ct1[:, b, :, :, 0:DK],
                                      crc[:, b].unsqueeze(3).broadcast_to([128, 4, 4, DK]), ALU.mult)\
                       .then_inc(sem(f"ct2{l}"), 1)
                for b in range(2):
                    after(dve, f"ct2{l}", p, b + 1, 2)
                    dve.transpose(ct3[:, l, b], ct2[:, b]).then_inc(sem(f"ct3{l}"), 1)

            def add_residual(l, p, turn):
                n = 1 if l == 0 else 3
                src = read(dve, "m", f"o{l}", turn)
                after(dve, f"res{n - 1}", p)
                free(dve.tensor_tensor(xs[n][:], src[:, 0:TOK].rearrange("p (b d) -> p b d", b=2), res[n - 1][:],
                                       ALU.add), "m", f"o{l}", turn)
                freed(dve, "m", f"o{l}", turn)

            def gelu_argument(n, i):
                after(dve, "fsq", i, n + 1, 2)
                h = slice(2 * n, 2 * n + 2)
                dve.scalar_tensor_tensor(fw[:, h], fs[:, h], 1.0, fv[:, h], ALU.add, ALU.mult).then_inc(sem("fw"), 1)

            def gelu_output(n, i):
                after(dve, "ftanh", i, n + 1, 2)
                h = slice(2 * n, 2 * n + 2)
                dve.scalar_tensor_tensor(fh[:, h], fs[:, h], 1.0, fv[:, h], ALU.add, ALU.mult).then_inc(sem("fh"), 1)

            def add_ffn(i):
                src = read(dve, "m", "ffy", i)
                after(dve, "res1", i)
                free(dve.tensor_tensor(xs[2][:], src[:, 0:TOK].rearrange("p (b d) -> p b d", b=2), res[1][:],
                                       ALU.add), "m", "ffy", i)
                freed(dve, "m", "ffy", i)

            def router_clamp(p):
                after(dve, "ss", p, of=2)
                dve.tensor_scalar(sc[:], ss[:], L2_EPS * L2_EPS, None, ALU.max).then_inc(sem("ss_clamped"), 1)

            def router_best(p, turn):
                src = read(dve, "m", "logit", turn)
                after(dve, "rn", p)
                for b in range(2):
                    ins = dve.tensor_scalar(lg[:, b], src[:, b * EXPERTS:(b + 1) * EXPERTS], rn[:, b:b + 1], None,
                                            ALU.mult)
                free(ins, "m", "logit", turn)
                freed(dve, "m", "logit", turn)
                dve.tensor_copy(tiny[:, 2:3], half[:, 0:1]).then_inc(sem("wait_carried"), 1)
                for b in range(2):
                    dve.max(top[:, b], lg[:, b]).then_inc(sem("top"), 1)
                after(dve, "top", p, of=2)
                dve.tensor_copy(tiny[:, 3:4], half[:, 0:1]).then_inc(sem("wait_carried"), 1)
                for b in range(2):
                    dve.match_replace(lr[:, b], top[:, b], lg[:, b], -1e30).then_inc(sem("lr"), 1)
                after(dve, "lr", p, of=2)
                dve.tensor_tensor(sel[:], lr[:], lg[:], ALU.not_equal).then_inc(sem("sel"), 1)

            def router_weights(p):
                after(dve, "sel", p)
                after(dve, "th", p)
                dve.scalar_tensor_tensor(sw[:], th[:], 1.0, sel[:], ALU.add, ALU.mult).then_inc(sem("sw"), 1)
                after(dve, "sw", p)
                dve.tensor_reduce(sws[:], sw[:], AX.X, ALU.add).then_inc(sem("sws"), 1)
                after(dve, "sws", p)
                dve.reciprocal(swr[:], sws[:]).then_inc(sem("swr"), 1)
                after(dve, "swr", p)
                for b in range(2):
                    dve.tensor_scalar(comb[:, b], sw[:, b], swr[:, b:b + 1], 0.5, ALU.mult, ALU.mult)\
                       .then_inc(sem("comb"), 1)
                after(dve, "comb", p, of=2)
                dve.tensor_copy(csp[:, :, 0], comb[:]).then_inc(sem("csp"), 1)
                after(dve, "csp", p, 1, 3)
                dve.tensor_tensor(cr[:], comb[:], csp[:, :, 0], ALU.subtract).then_inc(sem("cr"), 1)
                after(dve, "cr", p)
                dve.tensor_copy(csp[:, :, 1], cr[:]).then_inc(sem("csp"), 1)
                after(dve, "csp", p, 2, 3)
                dve.tensor_tensor(csp[:, :, 2], cr[:], csp[:, :, 1], ALU.subtract).then_inc(sem("csp"), 1)

            def gated(c, p, turn, between=None):
                rows = 128 if c < ECH else HID
                after(dve, "gth", p, c + 1, ECH + 1)
                src = read(dve, "s", f"gu{c}", turn) if c < ECH else read(dve, "m", "shared", turn)
                dve.scalar_tensor_tensor(ga[0:rows, c % 2], gth[0:rows, c % 4], 1.0, src[0:rows, 0:TOK],
                                         ALU.add, ALU.mult).then_inc(sem("ga"), 1)
                if between is not None:
                    weighted(between, p, turn)
                after(dve, "ga", p, c + 1, ECH + 1)
                if c < ECH:
                    free(dve.tensor_tensor(gb[:, c % 4], ga[:, c % 2], src[:, TOK:2 * TOK], ALU.mult),
                         "s", f"gu{c}", turn)
                else:
                    after(dve, "down", p, c - 1, ECH + 1)
                    free(dve.scalar_tensor_tensor(hT[0:rows, c % 2], ga[0:rows, c % 2], 0.5,
                                                  src[0:rows, TOK:2 * TOK], ALU.mult, ALU.mult), "m", "shared", turn)

            def weighted(c, p, turn):
                freed(dve, "s", f"gu{c}", turn)
                if c >= 2:
                    after(dve, "down", p, c - 1, ECH + 1)
                src = read(dve, "t", f"cb{c}", turn)
                free(dve.tensor_tensor(hT[:, c % 2], gb[:, c % 4], src[:, 0:TOK], ALU.mult), "t", f"cb{c}", turn)

            def output(p):
                dve.wait_ge(sem("stored"), 16 * (p + 1))
                after(dve, "down", p, of=ECH + 1)
                for b in range(2):
                    dve.tensor_tensor(xout[:, b], Y_BANK[:, b * D:(b + 1) * D], xs[3][:, b], ALU.add)\
                       .then_inc(sem("xout"), 1)

            dve.memset(nmw[:], 0.0).then_inc(sem("pads"), 1)
            dve.memset(cspw[:], 0.0).then_inc(sem("pads"), 1)
            dve.wait_ge(sem("half"), 1)
            after(dve, "x0_in", 0, of=16)
            variance(0, x0, 0)
            normalize(0, x0, 0)
            dve.memset(qst[0][:], 0.0).then_inc(sem("stacks_cleared"), 1)
            src = read(dve, "m", "rel0", "setup")
            free(dve.tensor_scalar(relrow[:], src[0:HEADS, 0:REL + 1], -1.0, None, ALU.mult), "m", "rel0", "setup")
            dve.wait_ge(sem("mask_in"), 16)
            dve.tensor_scalar(maskn[:], mask8[:], MASKED, None, ALU.mult).then_inc(sem("maskn"), 1)
            dve.memset(kst[1][:], 0.0).then_inc(sem("stacks_cleared"), 1)
            dve.memset(ones[:], 1.0).then_inc(sem("ones"), 1)
            dve.wait_ge(sem("maskn"), 1)
            dve.wait_ge(sem("biasq_in"), 32)
            v = biasq[:].rearrange("p a b k -> p (a b) k")
            dve.tensor_tensor(v, v, maskn[:].unsqueeze(1).broadcast_to([SEQ, HEADS, SEQ]), ALU.add)\
               .then_inc(sem("masked"), 1)
            dve.memset(va[:], 0.0).then_inc(sem("va_zeros"), 1)
            dve.wait_ge(sem("va_zeros"), 1)
            dve.memset(va[:, :, :, :, DK:DK + 1], 1.0).then_inc(sem("va_cleared"), 1)
            dve.wait_ge(sem("ident_in"), 16)
            dve.tensor_copy(identb[:], ident[:]).then_inc(sem("identb"), 1)
            dve.wait_ge(sem("gsq"), 1)
            dve.tensor_scalar(gss[:, 0:1], gss[:, 0:1], L2_EPS * L2_EPS, None, ALU.max).then_inc(sem("gss"), 1)
            dve.wait_ge(sem("gate_norm"), 1)
            dve.tensor_scalar(gsq[:], gate[:], gss[:, 1:2], None, ALU.mult).then_inc(sem("gate_normed"), 1)
            free(dve.tensor_copy(w1[:], read(dve, "m", "w1", "setup")[:]), "m", "w1", "setup")
            free(dve.tensor_scalar(w2[:], read(dve, "m", "w2", "setup")[:].rearrange("p (n d) -> p n d", n=FCH),
                                   0.5, None, ALU.mult), "m", "w2", "setup")
            free(dve.tensor_copy(gateT[:], read(dve, "m", "gateT", "setup")[:, 0:EXPERTS]), "m", "gateT", "setup")
            dve.wait_ge(sem("masked"), 1)
            dve.wait_ge(sem("pads"), 2)

            def body(i):
                p = i - 1
                first = isinstance(i, int) and i == 0
                last = isinstance(i, int) and i == PAIRS - 1
                row_max0(0, i)
                if not last:
                    after(dve, "x0_in", i + 1, of=16)
                    variance(0, x0, i + 1)
                    normalize(0, x0, i + 1)
                if not first:
                    row_max1(0, p, i)
                    row_max1(1, p, i)
                row_max0(1, i)
                if first:
                    dve.wait_ge(sem("expsel_in"), 16)
                    dve.tensor_copy(expsel[:], expself[:]).then_inc(sem("expsel"), 1)
                if not first:
                    context(1, p, i)
                    add_residual(1, p, i)
                    variance(3, xs[3], p)
                    normalize(3, xs[3], p)
                context(0, i, i)
                if not first:
                    router_clamp(p)
                add_residual(0, i, i)
                variance(1, xs[1], i)
                if not first:
                    router_best(p, i)
                normalize(1, xs[1], i)
                if not first:
                    router_weights(p)
                    gated(0, p, i)
                    gated(1, p, i)
                gelu_argument(0, i)
                gelu_argument(1, i)
                if not first:
                    weighted(0, p, i)
                    gated(2, p, i, between=1)
                gelu_output(0, i)
                gelu_output(1, i)
                if not first:
                    gated(3, p, i, between=2)
                add_ffn(i)
                variance(2, xs[2], i)
                if not first:
                    weighted(3, p, i)
                normalize(2, xs[2], i)
                if not first:
                    gated(4, p, i)
                    for c in range(5, ECH + 1):
                        gated(c, p, i, between=c - 1)
                    output(p)

            body(0)
            with dve.Fori(1, PAIRS - 1) as i:
                body(i)
            body(PAIRS - 1)
            p = PAIRS - 1
            row_max1(0, p, "tail")
            row_max1(1, p, "tail")
            context(1, p, "tail")
            add_residual(1, p, "tail")
            variance(3, xs[3], p)
            normalize(3, xs[3], p)
            router_clamp(p)
            router_best(p, "tail")
            router_weights(p)
            gated(0, p, "tail")
            gated(1, p, "tail")
            weighted(0, p, "tail")
            for c in range(2, ECH + 1):
                gated(c, p, "tail", between=c - 1)
            output(p)

        @block.tensor
        def _(pe):
            def turn_tokens(n, name, i, turn):
                after(pe, f"xn{n}", i, of=2)
                dst = fill(pe, "m", name, turn)
                for b in range(2):
                    ins = pe.transpose(dst[:, b * SEQ:(b + 1) * SEQ], xn[n][:, b], ident[:])
                filled(ins, "m", name, turn)

            def turn_front(p, turn):
                after(pe, "xn0", p, of=2)
                after(pe, "cx_in", p, of=16)
                dst = fill(pe, "m", "xcT", turn)
                for k, src in enumerate((xn[0], cx)):
                    for b in range(2):
                        t = (2 * k + b) * SEQ
                        ins = pe.transpose(dst[:, t:t + SEQ], src[:, b], ident[:])
                filled(ins, "m", "xcT", turn)

            def keys(l, turn):
                freed(pe, "m", "xcT", turn)
                dst = fill(pe, "m", f"k{l}", turn)
                filled(pe.matmul(dst[:, 0:TOK], wqk[:, l, 1], xcT[:, 1], start=True, stop=True), "m", f"k{l}", turn)

            def queries(l, turn):
                freed(pe, "m", "xn2T" if l else "xcT", turn)
                dst = fill(pe, "m", f"q{l}", turn)
                ins = pe.matmul(dst[:, 0:TOK], wqk[:, l, 0], xnT[2][:] if l else xcT[:, 0], start=True, stop=True)
                filled(ins, "m", f"q{l}", turn)

            def value_rows(b, turn):
                dst = fill(pe, "m", f"v{b}", turn)
                filled(pe.matmul(dst[:, 0:TOK], xcT[:, 1, b * SEQ:(b + 1) * SEQ], wv[:], start=True, stop=True),
                       "m", f"v{b}", turn)

            def scores(l, b, cs, p, turn):
                if b == 0 and 0 in cs:
                    for name in (f"kst{l}", f"qst{l}"):
                        after(pe, f"{name}_in", p, of=16 * STACK_DMAS[name])
                for c in cs:
                    dst = fill(pe, "s", f"S{l}{b}{c}", turn)
                    tok = slice(b * SEQ, (b + 1) * SEQ)
                    for hp in (2 * c, 2 * c + 1):
                        at = 2 * (hp - 2 * c) * SEQ
                        if l == 1:
                            ins = pe.matmul(dst[:, at:at + 2 * SEQ].rearrange("p (h k) -> p h k", h=2),
                                            qst[1][0:SROWS, hp, tok], kst[1][0:SROWS, hp, :, tok],
                                            start=True, stop=True)
                        else:
                            for hh in range(2):
                                ins = pe.matmul(dst[:, at + hh * SEQ:at + (hh + 1) * SEQ],
                                                qst[0][:, hp, hh, tok], kst[0][:, hp, tok], start=True, stop=True)
                    filled(ins, "s", f"S{l}{b}{c}", turn)

            def turn_max(b, p, turn):
                after(pe, f"nm1{b}", p)
                dst = fill(pe, "m", f"nmT1{b}", turn)
                ins = pe.transpose(dst[:].bitcast(BF16)[:, 0:SEQ], nmw[:, b], identb[:])
                filled(ins, "m", f"nmT1{b}", turn)

            def turn_weights0(b, cs, i):
                for c in cs:
                    after(pe, f"p0{b}", i, c + 1, 4)
                    dst = fill(pe, "t", f"T0{b}{c}", i)
                    for s in range(4):
                        ins = pe.transpose(dst[:, s * SEQ:(s + 1) * SEQ], es[:, b, 4 * c + s], ident[:])
                    filled(ins, "t", f"T0{b}{c}", i)

            def scores1_turned(b, p, turn):
                after(pe, f"max1{b}_in", p, of=16)
                for c in range(4):
                    dst = fill(pe, "t", f"T1{b}{c}", turn)
                    tok = slice(b * SEQ, (b + 1) * SEQ)
                    for s in range(4):
                        hp, hh = 2 * c + s // 2, s % 2
                        ins = pe.matmul(dst[:, s * SEQ:(s + 1) * SEQ], kst[1][:, hp, hh, tok],
                                        qst[1][:, hp, tok], start=True, stop=True)
                    filled(ins, "t", f"T1{b}{c}", turn)

            def values(l, b, p, turn):
                if b == 0:
                    after(pe, f"va{l}", p)
                dst = fill(pe, "m", f"C{l}{b}", turn)
                for c in range(4):
                    freed(pe, "t", f"T{l}{b}{c}", turn)
                    for s in range(4 * c, 4 * c + 4):
                        head = HALF * (s % 2) + s // 2
                        j, g = head // 4, head % 4
                        ins = pe.matmul(dst[32 * j:32 * j + VW, g * SEQ:(g + 1) * SEQ], va[:, l, b, head],
                                        pt[:, l, b, s], start=True, stop=True)
                filled(ins, "m", f"C{l}{b}", turn)

            def attention_out(l, p, turn):
                after(pe, f"ct3{l}", p, of=2)
                dst = fill(pe, "m", f"o{l}", turn)
                for b in range(2):
                    ins = pe.matmul(dst[:, b * D:(b + 1) * D], ct3[:, l, b], wo[:, l], start=True, stop=True)
                filled(ins, "m", f"o{l}", turn)

            def ffn_up(n, i):
                if n == 0:
                    freed(pe, "m", "xn1T", i)
                dst = fill(pe, "m", f"ff{n}", i)
                for k in range(2):
                    f = 2 * n + k
                    ins = pe.matmul(dst[:, k * TOK:(k + 1) * TOK], w1[:, f * 128:(f + 1) * 128], xnT[1][:],
                                    start=True, stop=True)
                filled(ins, "m", f"ff{n}", i)

            def ffn_down(i):
                dst = fill(pe, "m", "ffy", i)
                for f in range(FCH):
                    if f % 2 == 0:
                        after(pe, "fh", i, f // 2 + 1, 2)
                    for b in range(2):
                        ins = pe.matmul(dst[:, b * D:(b + 1) * D], fh[:, f, b * SEQ:(b + 1) * SEQ], w2[:, f],
                                        start=(f == 0 and b == 0), stop=(f == FCH - 1), skip_group_check=True)
                filled(ins, "m", "ffy", i)

            def logits(turn):
                freed(pe, "m", "xn3T", turn)
                dst = fill(pe, "m", "logit", turn)
                for b in range(2):
                    ins = pe.matmul(dst[:, b * EXPERTS:(b + 1) * EXPERTS], xnT[3][:, b * SEQ:(b + 1) * SEQ], gateT[:],
                                    start=True, stop=True)
                filled(ins, "m", "logit", turn)

            def gate_up(c, turn):
                ring, name = ("s", f"gu{c}") if c < ECH else ("m", "shared")
                rows = 128 if c < ECH else HID
                dst = fill(pe, ring, name, turn)
                for k, w in enumerate((wg, wu)):
                    ins = pe.matmul(dst[0:rows, k * TOK:(k + 1) * TOK], w[:, c * 128:c * 128 + rows], xnT[3][:],
                                    start=True, stop=True)
                filled(ins, ring, name, turn)

            def turn_weights(p, turn):
                after(pe, "csp", p, of=3)
                dst = fill(pe, "m", "combT", turn)
                for b in range(2):
                    ins = pe.transpose(dst[:].bitcast(BF16)[:, b * SEQ:(b + 1) * SEQ], cspw[:, b], identb[:])
                filled(ins, "m", "combT", turn)

            def spread(c, turn):
                dst = fill(pe, "t", f"cb{c}", turn)
                filled(pe.matmul(dst[:, 0:TOK], expsel[:, c], combT[:], start=True, stop=True), "t", f"cb{c}", turn)

            def down(c, p, turn):
                rows = 128 if c < ECH else HID
                freed(pe, *(("t", f"cb{c}") if c < ECH else ("m", "shared")), turn)
                for b in range(2):
                    ins = pe.matmul(Y_BANK[:, b * D:(b + 1) * D], hT[0:rows, c % 2, b * SEQ:(b + 1) * SEQ],
                                    wd[:, c] if c < ECH else swd[:], start=(c == 0 and b == 0), stop=(c == ECH),
                                    skip_group_check=True)
                ins.then_inc(sem("down"), 1)

            pe.wait_ge(sem("ident_in"), 16)
            turn_front(0, "setup")
            pe.wait_ge(sem("rel_in"), 32)
            dst = fill(pe, "m", "rel0", "setup")
            ins = pe.matmul(dst[0:HEADS, 0:REL + 1], table[:], onehot[:], start=True, stop=True)
            filled(ins, "m", "rel0", "setup")
            pe.wait_ge(sem("wqk_in"), 16)
            keys(0, "setup")
            keys(1, "setup")
            queries(0, "setup")
            pe.wait_ge(sem("wv_in"), 16)
            value_rows(0, "setup")
            value_rows(1, "setup")

            pe.wait_ge(sem("ffw_in"), 64)
            dst = fill(pe, "m", "w1", "setup")
            filled(pe.matmul(dst[:], u1t[:], v1[:], start=True, stop=True), "m", "w1", "setup")
            dst = fill(pe, "m", "w2", "setup")
            for n in range(FCH):
                ins = pe.matmul(dst[:, n * D:(n + 1) * D], u2t[:, n * 128:(n + 1) * 128], v2[:], start=True, stop=True)
            filled(ins, "m", "w2", "setup")
            pe.wait_ge(sem("gate_normed"), 1)
            dst = fill(pe, "m", "gateT", "setup")
            filled(pe.transpose(dst[:, 0:EXPERTS], gsq[:], ident[0:EXPERTS, 0:EXPERTS]), "m", "gateT", "setup")
            pe.wait_ge(sem("identb"), 1)

            def body(i):
                p = i - 1
                first = isinstance(i, int) and i == 0
                last = isinstance(i, int) and i == PAIRS - 1
                scores(0, 0, range(4), i, i)
                turn_weights0(0, (0, 1), i)
                if first:
                    scores(0, 1, (0, 1), i, i)
                if not first:
                    scores(1, 0, (0, 1), p, i)
                turn_weights0(0, (2,), i)
                if not first:
                    scores(1, 0, (2, 3), p, i)
                turn_weights0(0, (3,), i)
                if first:
                    scores(0, 1, (2, 3), i, i)
                    values(0, 0, i, i)
                if not last:
                    turn_front(i + 1, i)
                if not first:
                    scores(1, 1, (0, 1), p, i)
                    turn_max(0, p, i)
                    if not last:
                        keys(0, i)
                    scores(1, 1, (2, 3), p, i)
                    if not last:
                        keys(1, i)
                        queries(0, i)
                    scores(0, 1, (0, 1), i, i)
                    turn_max(1, p, i)
                    scores1_turned(0, p, i)
                    scores(0, 1, (2, 3), i, i)
                    values(1, 0, p, i)
                    scores1_turned(1, p, i)
                    values(1, 1, p, i)
                turn_weights0(1, (0, 1), i)
                if not first:
                    attention_out(1, p, i)
                turn_weights0(1, (2, 3), i)
                if not first:
                    values(0, 0, i, i)
                values(0, 1, i, i)
                if first:
                    keys(0, i)
                    keys(1, i)
                    queries(0, i)
                if not first:
                    turn_tokens(3, "xn3T", p, i)
                    logits(i)
                if first:
                    pe.wait_ge(sem("wo_in"), 16)
                attention_out(0, i, i)
                if not last:
                    value_rows(0, i)
                if not first:
                    gate_up(0, i)
                    gate_up(1, i)
                if not last:
                    value_rows(1, i)
                turn_tokens(1, "xn1T", i, i)
                ffn_up(0, i)
                ffn_up(1, i)
                if not first:
                    turn_weights(p, i)
                    gate_up(2, i)
                    freed(pe, "m", "combT", i)
                    spread(0, i)
                    spread(1, i)
                    gate_up(3, i)
                    down(0, p, i)
                    spread(2, i)
                    down(1, p, i)
                    spread(3, i)
                    gate_up(4, i)
                ffn_down(i)
                if not first:
                    down(2, p, i)
                    gate_up(5, i)
                    spread(4, i)
                turn_tokens(2, "xn2T", i, i)
                if not first:
                    down(3, p, i)
                    spread(5, i)
                queries(1, i)
                if not first:
                    for c in range(6, ECH):
                        gate_up(c, i)
                        down(c - 2, p, i)
                        spread(c, i)
                    gate_up(ECH, i)
                    for c in range(ECH - 2, ECH + 1):
                        down(c, p, i)

            body(0)
            pe.wait_ge(sem("kst_ones"), 32)
            pe.wait_ge(sem("moe_in"), 64)
            pe.wait_ge(sem("expsel"), 1)
            with pe.Fori(1, PAIRS - 1) as i:
                body(i)
            body(PAIRS - 1)
            p = PAIRS - 1
            scores(1, 0, range(4), p, "tail")
            scores(1, 1, (0, 1), p, "tail")
            turn_max(0, p, "tail")
            scores(1, 1, (2, 3), p, "tail")
            scores1_turned(0, p, "tail")
            turn_max(1, p, "tail")
            values(1, 0, p, "tail")
            scores1_turned(1, p, "tail")
            values(1, 1, p, "tail")
            attention_out(1, p, "tail")
            turn_tokens(3, "xn3T", p, "tail")
            logits("tail")
            gate_up(0, "tail")
            gate_up(1, "tail")
            turn_weights(p, "tail")
            gate_up(2, "tail")
            freed(pe, "m", "combT", "tail")
            spread(0, "tail")
            spread(1, "tail")
            for c in range(3, ECH + 3):
                if c <= ECH:
                    gate_up(c, "tail")
                down(c - 3, p, "tail")
                if c - 1 < ECH:
                    spread(c - 1, "tail")
            down(ECH, p, "tail")


def bucket_onehot():
    behind = np.maximum(np.arange(REL) - (SEQ - 1), 0)
    exact = BUCKETS // 2
    f = np.maximum(behind, 1).astype(np.float32)
    large = exact + (np.log(f / np.float32(exact)) / np.float32(np.log(MAX_DISTANCE / exact))
                     * np.float32(BUCKETS - exact)).astype(np.int32)
    bucket = np.where(behind < exact, behind, np.minimum(large, BUCKETS - 1))
    out = np.zeros((BUCKETS, REL + 1), np.float32)
    out[bucket, np.arange(REL)] = 1.0
    return out


def expert_selector():
    out = np.zeros((3, EXPERTS, ECH, 128), np.float32)
    for e in range(EXPERTS):
        first = e * HID
        out[:, e, first // 128, first % 128:first % 128 + HID] = 1.0
    return out.reshape(3 * EXPERTS, ECH, 128)


def kernel(**inputs):
    import numpy as _np
    import concourse.bacc as _bacc
    from concourse import mybir as _mybir
    from concourse.bass_utils import run_bass_kernel_spmd as _run

    a = {k: _np.asarray(v) for k, v in inputs.items()}
    heads_in = lambda w: w.transpose(1, 0, 2).reshape(D, D)
    wq1, wk1, wv1 = (heads_in(a[f"L1_xattn_W{c}"]) for c in "qkv")
    by_dim = lambda w: w.reshape(-1, 2, HALF, DK).swapaxes(2, 3).reshape(w.shape)
    experts_in = lambda w: w.transpose(1, 0, 2).reshape(D, EXPERTS * HID)
    arrays = {
        "x": a["x"],
        "ctx": a["ctx_1024"][:, ::-1],
        "mask": a["mask_1x1xSxS2_bk1"].reshape(SEQ, SEQ)[:, ::-1].view(_np.uint8),
        "wqk": _np.stack([_np.stack([by_dim(a["L0_xattn_Wq"]), by_dim(a["L0_xattn_Wk"])], 1),
                          _np.stack([by_dim(wq1), by_dim(wk1)], 1)], 1),
        "wv": _np.stack([a["L0_xattn_Wv"], wv1], 1),
        "wo": _np.stack([a["L0_xattn_Wo"], a["L1_xattn_Wo"]], 1),
        "bqk": _np.stack([by_dim(a[f"L{l}_xattn_b{c}"].reshape(D)) for l in range(2) for c in "qk"], 1),
        "bv": _np.tile(_np.concatenate([a["L0_xattn_bv"], a["L1_xattn_bv"].reshape(D)]), (2, 1)),
        "rows": _np.stack([_np.tile(a[n], (2, 1)) for n in ("L0_xattn_bo", "L0_ffn_b2", "L1_xattn_bo")]),
        "table": a["L0_xattn_rpe_table"],
        "u1t": a["L0_ffn_U1"].T,
        "v1": a["L0_ffn_V1"],
        "b1": a["L0_ffn_b1"].reshape(FCH, 128).T,
        "u2t": a["L0_ffn_U2"].T,
        "v2": a["L0_ffn_V2"],
        "gate": a["L1_ffn_gate_w"],
        "wg": _np.concatenate([experts_in(a["L1_ffn_w_gate"]), a["L1_ffn_sw_gate"]], 1),
        "wu": _np.concatenate([experts_in(a["L1_ffn_w_up"]), a["L1_ffn_sw_up"]], 1),
        "wd": a["L1_ffn_w_down"].reshape(ECH, 128, D).transpose(1, 0, 2),
        "swd": a["L1_ffn_sw_down"],
        "ident": _np.eye(128, dtype=_np.float32),
        "onehot": bucket_onehot(),
        "expsel": expert_selector(),
    }
    arrays = {f"in_{k}": _np.ascontiguousarray(v) for k, v in arrays.items()}
    nc = _bacc.Bacc("TRN2", target_bir_lowering=False, num_devices=1)
    args = [nc.dram_tensor(k, v.shape, _mybir.dt.from_np(v.dtype), kind="ExternalInput").ap() for k, v in arrays.items()]
    args.append(nc.dram_tensor("out_0", (BATCH, SEQ, D), _mybir.dt.float32, kind="ExternalOutput").ap())
    bass_xattn_ffn_moe(nc, *args)
    r = _run(nc, [arrays], core_ids=[0])
    return r.results[0]["out_0"]
```
